# Optimizing a Trainium2 kernel written in Bass

```python
import numpy as np
import jax
import jax.numpy as jnp

def _softmax(x, axis=-1):
    return jax.nn.softmax(x, axis=axis)

def _gelu(x):
    return jax.nn.gelu(x, approximate=True)

def _silu(x):
    return jax.nn.silu(x)

def _sigmoid(x):
    return jax.nn.sigmoid(x)

def _layernorm(x, axis=-1, eps=1e-05):
    m = jnp.mean(x, axis=axis, keepdims=True)
    v = jnp.var(x, axis=axis, keepdims=True)
    return (x - m) / jnp.sqrt(v + eps)

def _scatter_add(tgt, idx, src, axis=0):
    return tgt.at[idx].add(src)

def _segment_sum(src, seg, n):
    return jax.ops.segment_sum(src, seg, n)
kernel_name = 'mk_xattn_ffn_d1_seqx_r8_c887e4'

def setup_inputs(seed: int=0):
    np.random.seed(seed)
    _w = jnp.asarray

    def _rec_inputs():
        import jax
        import jax.numpy as jnp
        _rk = jax.random.key(seed)
        x = -0.000125 + 0.9999 * jax.random.normal(jax.random.fold_in(_rk, 1), (8, 256, 256), jnp.float32)
        _lenS = 256 - jax.random.randint(jax.random.fold_in(_rk, 7), (8,), 0, max(1, 256 // 4) + 1, jnp.int32)
        _lenS2 = 1601 - jax.random.randint(jax.random.fold_in(_rk, 8), (8,), 0, max(1, 1601 // 4) + 1, jnp.int32)
        _ctx_2048P = jax.random.normal(jax.random.fold_in(_rk, 11), (8, 16, 256), jnp.float32)
        _ctx_2048c = jax.random.dirichlet(jax.random.fold_in(_rk, 511), 0.3 * jnp.ones((16,), jnp.float32), (8, 1601))
        _ctx_2048t = jnp.einsum('bsk,bkd->bsd', _ctx_2048c, _ctx_2048P)
        _ctx_2048t = _ctx_2048t * jax.lax.rsqrt(jnp.mean(jnp.square(_ctx_2048t)) + 1e-12) * 0.953939
        ctx_2048 = -0.000540021 + 0.99982 * (_ctx_2048t + 0.3 * jax.random.normal(jax.random.fold_in(_rk, 611), (8, 1601, 256), jnp.float32))
        return (x, ctx_2048)
    x, ctx_2048 = _rec_inputs()

    def _L0_xattn_setup():
        import jax, jax.numpy as jnp
        import numpy as np
        DIM = 256
        N_HEADS = 16
        HEAD_DIM = DIM // N_HEADS
        EPS = 1e-06
        IMG_LEN = 257

        def rms_norm(x, g, eps=EPS):
            var = jnp.mean(x * x, axis=-1, keepdims=True)
            return x * jax.lax.rsqrt(var + eps) * g

        def _attend(q, k, v, k_mask=None):
            scale = 1.0 / jnp.sqrt(jnp.asarray(HEAD_DIM, q.dtype))
            scores = jnp.einsum('bqnd,bknd->bnqk', q, k) * scale
            if k_mask is not None:
                neg = jnp.asarray(jnp.finfo(scores.dtype).min, scores.dtype)
                scores = jnp.where(k_mask[:, None, None, :], scores, neg)
            probs = jax.nn.softmax(scores, axis=-1)
            return jnp.einsum('bnqk,bknd->bqnd', probs, v)
        key = jax.random.key(seed)
        ks = jax.random.split(key, 16)
        B, L1, L2 = (1, 2048, 769)
        std = 0.02
        inp = {'x': jax.random.normal(ks[0], (B, L1, DIM), jnp.float32), 'context': jax.random.normal(ks[1], (B, L2, DIM), jnp.float32), 'context_lens': jax.random.randint(ks[2], (B,), 32, 513, jnp.int32), 'Wq': jax.random.normal(ks[3], (DIM, DIM), jnp.float32) * std, 'bq': jnp.zeros((DIM,), jnp.float32), 'gq': jnp.ones((DIM,), jnp.float32), 'Wk': jax.random.normal(ks[4], (DIM, DIM), jnp.float32) * std, 'bk': jnp.zeros((DIM,), jnp.float32), 'gk': jnp.ones((DIM,), jnp.float32), 'Wv': jax.random.normal(ks[5], (DIM, DIM), jnp.float32) * std, 'bv': jnp.zeros((DIM,), jnp.float32), 'Wk_img': jax.random.normal(ks[6], (DIM, DIM), jnp.float32) * std, 'bk_img': jnp.zeros((DIM,), jnp.float32), 'gk_img': jnp.ones((DIM,), jnp.float32), 'Wv_img': jax.random.normal(ks[7], (DIM, DIM), jnp.float32) * std, 'bv_img': jnp.zeros((DIM,), jnp.float32), 'Wo': jax.random.normal(ks[8], (DIM, DIM), jnp.float32) * std, 'bo': jnp.zeros((DIM,), jnp.float32)}
        return inp
    _L0_xattn_all = _L0_xattn_setup()
    _L0_xattn_in = {k: v for k, v in _L0_xattn_all.items() if k in ('context_lens', 'Wq', 'bq', 'gq', 'Wk', 'bk', 'gk', 'Wv', 'bv', 'Wk_img', 'bk_img', 'gk_img', 'Wv_img', 'bv_img', 'Wo', 'bo')}
    del _L0_xattn_all

    def _L0_ffn_setup():
        import jax, jax.numpy as jnp
        import numpy as np
        B, S, H, I, E, F, K, R, TOPK = (1, 128, 256, 176, 64, 8, 8, 8, 6)
        ISH = 2 * I

        def _fused_linear(x, W, qa, qb, scale, w):
            out = x @ W.T
            a = jnp.einsum('th,krh->tkr', x, qa)
            b = jnp.einsum('tkr,khr->tkh', a, qb)
            mix = jnp.einsum('tkh,tk->th', b, w)
            return out + scale[None, :] * mix

        def _moe_forward(hidden_states, gate_weight, inv_mapping, mask_up_W, gate_W, gate_qa, gate_qb, gate_scale, up_W, up_qa, up_qb, up_scale, down_W, down_qa, down_qb, down_scale, sh_gate_W, sh_up_W, sh_down_W):
            b, s, h = hidden_states.shape
            x = hidden_states.reshape(-1, h)
            T = x.shape[0]
            scores = jax.nn.softmax(x @ gate_weight.T, axis=-1)
            topk_w, topk_idx = jax.lax.top_k(scores, TOPK)
            w_dense = jnp.zeros((T, E), x.dtype).at[jnp.arange(T)[:, None], topk_idx].add(topk_w)
            flat = w_dense[:, inv_mapping]
            scalar = flat.sum(-1)
            soft = jax.nn.softmax(jnp.where(flat == 0, -1000000000.0, flat), axis=-1)

            def expert(muW, gW, gqa, gqb, gs, uW, uqa, uqb, us, dW, dqa, dqb, ds, w):
                xe = x + w @ muW.T
                gate = jax.nn.silu(_fused_linear(xe, gW, gqa, gqb, gs, w))
                up = _fused_linear(xe, uW, uqa, uqb, us, w)
                return _fused_linear(gate * up, dW, dqa, dqb, ds, w)
            outs = jax.vmap(expert, in_axes=(0,) * 13 + (1,))(mask_up_W, gate_W, gate_qa, gate_qb, gate_scale, up_W, up_qa, up_qb, up_scale, down_W, down_qa, down_qb, down_scale, soft)
            y = jnp.einsum('fth,tf->th', outs, scalar).reshape(b, s, h)
            sh = jax.nn.silu(hidden_states @ sh_gate_W.T) * (hidden_states @ sh_up_W.T) @ sh_down_W.T
            return y + sh
        key = jax.random.key(seed)
        ks = jax.random.split(key, 20)
        g = lambda k, shape, s=0.02: jax.random.normal(k, shape, jnp.float32) * s
        return {'hidden_states': jax.random.normal(ks[0], (B, S, H), jnp.float32), 'gate_weight': g(ks[1], (E, H)), 'inv_mapping': jnp.arange(E, dtype=jnp.int32).reshape(F, K), 'mask_up_W': g(ks[2], (F, H, K)), 'gate_W': g(ks[3], (F, I, H)), 'gate_qa': g(ks[4], (F, K, R, H)), 'gate_qb': g(ks[5], (F, K, I, R)), 'gate_scale': jnp.full((F, I), 0.1, jnp.float32), 'up_W': g(ks[6], (F, I, H)), 'up_qa': g(ks[7], (F, K, R, H)), 'up_qb': g(ks[8], (F, K, I, R)), 'up_scale': jnp.full((F, I), 0.1, jnp.float32), 'down_W': g(ks[9], (F, H, I)), 'down_qa': g(ks[10], (F, K, R, I)), 'down_qb': g(ks[11], (F, K, H, R)), 'down_scale': jnp.full((F, H), 0.1, jnp.float32), 'sh_gate_W': g(ks[12], (ISH, H)), 'sh_up_W': g(ks[13], (ISH, H)), 'sh_down_W': g(ks[14], (H, ISH))}
    _L0_ffn_all = _L0_ffn_setup()
    _L0_ffn_in = {k: v for k, v in _L0_ffn_all.items() if k in ('gate_weight', 'inv_mapping', 'mask_up_W', 'gate_W', 'gate_qa', 'gate_qb', 'gate_scale', 'up_W', 'up_qa', 'up_qb', 'up_scale', 'down_W', 'down_qa', 'down_qb', 'down_scale', 'sh_gate_W', 'sh_up_W', 'sh_down_W')}
    del _L0_ffn_all
    return {'x': x, 'ctx_2048': ctx_2048, 'L0_xattn_context_lens': _L0_xattn_in['context_lens'], 'L0_xattn_Wq': _L0_xattn_in['Wq'], 'L0_xattn_bq': _L0_xattn_in['bq'], 'L0_xattn_gq': _L0_xattn_in['gq'], 'L0_xattn_Wk': _L0_xattn_in['Wk'], 'L0_xattn_bk': _L0_xattn_in['bk'], 'L0_xattn_gk': _L0_xattn_in['gk'], 'L0_xattn_Wv': _L0_xattn_in['Wv'], 'L0_xattn_bv': _L0_xattn_in['bv'], 'L0_xattn_Wk_img': _L0_xattn_in['Wk_img'], 'L0_xattn_bk_img': _L0_xattn_in['bk_img'], 'L0_xattn_gk_img': _L0_xattn_in['gk_img'], 'L0_xattn_Wv_img': _L0_xattn_in['Wv_img'], 'L0_xattn_bv_img': _L0_xattn_in['bv_img'], 'L0_xattn_Wo': _L0_xattn_in['Wo'], 'L0_xattn_bo': _L0_xattn_in['bo'], 'L0_ffn_gate_weight': _L0_ffn_in['gate_weight'], 'L0_ffn_inv_mapping': _L0_ffn_in['inv_mapping'], 'L0_ffn_mask_up_W': _L0_ffn_in['mask_up_W'], 'L0_ffn_gate_W': _L0_ffn_in['gate_W'], 'L0_ffn_gate_qa': _L0_ffn_in['gate_qa'], 'L0_ffn_gate_qb': _L0_ffn_in['gate_qb'], 'L0_ffn_gate_scale': _L0_ffn_in['gate_scale'], 'L0_ffn_up_W': _L0_ffn_in['up_W'], 'L0_ffn_up_qa': _L0_ffn_in['up_qa'], 'L0_ffn_up_qb': _L0_ffn_in['up_qb'], 'L0_ffn_up_scale': _L0_ffn_in['up_scale'], 'L0_ffn_down_W': _L0_ffn_in['down_W'], 'L0_ffn_down_qa': _L0_ffn_in['down_qa'], 'L0_ffn_down_qb': _L0_ffn_in['down_qb'], 'L0_ffn_down_scale': _L0_ffn_in['down_scale'], 'L0_ffn_sh_gate_W': _L0_ffn_in['sh_gate_W'], 'L0_ffn_sh_up_W': _L0_ffn_in['sh_up_W'], 'L0_ffn_sh_down_W': _L0_ffn_in['sh_down_W']}

def reference(x, ctx_2048, L0_xattn_context_lens, L0_xattn_Wq, L0_xattn_bq, L0_xattn_gq, L0_xattn_Wk, L0_xattn_bk, L0_xattn_gk, L0_xattn_Wv, L0_xattn_bv, L0_xattn_Wk_img, L0_xattn_bk_img, L0_xattn_gk_img, L0_xattn_Wv_img, L0_xattn_bv_img, L0_xattn_Wo, L0_xattn_bo, L0_ffn_gate_weight, L0_ffn_inv_mapping, L0_ffn_mask_up_W, L0_ffn_gate_W, L0_ffn_gate_qa, L0_ffn_gate_qb, L0_ffn_gate_scale, L0_ffn_up_W, L0_ffn_up_qa, L0_ffn_up_qb, L0_ffn_up_scale, L0_ffn_down_W, L0_ffn_down_qa, L0_ffn_down_qb, L0_ffn_down_scale, L0_ffn_sh_gate_W, L0_ffn_sh_up_W, L0_ffn_sh_down_W):
    import jax
    import jax.numpy as jnp

    def _L0_xattn_ref(x, context, context_lens, Wq, bq, gq, Wk, bk, gk, Wv, bv, Wk_img, bk_img, gk_img, Wv_img, bv_img, Wo, bo):
        import jax, jax.numpy as jnp
        import numpy as np
        DIM = 256
        N_HEADS = 16
        HEAD_DIM = DIM // N_HEADS
        EPS = 1e-06
        IMG_LEN = 257

        def rms_norm(x, g, eps=EPS):
            var = jnp.mean(x * x, axis=-1, keepdims=True)
            return x * jax.lax.rsqrt(var + eps) * g

        def _attend(q, k, v, k_mask=None):
            scale = 1.0 / jnp.sqrt(jnp.asarray(HEAD_DIM, q.dtype))
            scores = jnp.einsum('bqnd,bknd->bnqk', q, k) * scale
            if k_mask is not None:
                neg = jnp.asarray(jnp.finfo(scores.dtype).min, scores.dtype)
                scores = jnp.where(k_mask[:, None, None, :], scores, neg)
            probs = jax.nn.softmax(scores, axis=-1)
            return jnp.einsum('bnqk,bknd->bqnd', probs, v)
        b = x.shape[0]
        n, d = (N_HEADS, HEAD_DIM)
        ctx_img = context[:, :IMG_LEN]
        ctx_txt = context[:, IMG_LEN:]
        q = rms_norm(x @ Wq + bq, gq).reshape(b, -1, n, d)
        k = rms_norm(ctx_txt @ Wk + bk, gk).reshape(b, -1, n, d)
        v = (ctx_txt @ Wv + bv).reshape(b, -1, n, d)
        k_img = rms_norm(ctx_img @ Wk_img + bk_img, gk_img).reshape(b, -1, n, d)
        v_img = (ctx_img @ Wv_img + bv_img).reshape(b, -1, n, d)
        img_x = _attend(q, k_img, v_img)
        k_mask = jnp.arange(k.shape[1])[None, :] < context_lens[:, None]
        txt_x = _attend(q, k, v, k_mask)
        out = (txt_x + img_x).reshape(b, -1, n * d)
        return out @ Wo + bo

    def _L0_ffn_ref(hidden_states, gate_weight, inv_mapping, mask_up_W, gate_W, gate_qa, gate_qb, gate_scale, up_W, up_qa, up_qb, up_scale, down_W, down_qa, down_qb, down_scale, sh_gate_W, sh_up_W, sh_down_W):
        import jax, jax.numpy as jnp
        import numpy as np
        B, S, H, I, E, F, K, R, TOPK = (1, 128, 256, 176, 64, 8, 8, 8, 6)
        ISH = 2 * I

        def _fused_linear(x, W, qa, qb, scale, w):
            out = x @ W.T
            a = jnp.einsum('th,krh->tkr', x, qa)
            b = jnp.einsum('tkr,khr->tkh', a, qb)
            mix = jnp.einsum('tkh,tk->th', b, w)
            return out + scale[None, :] * mix

        def _moe_forward(hidden_states, gate_weight, inv_mapping, mask_up_W, gate_W, gate_qa, gate_qb, gate_scale, up_W, up_qa, up_qb, up_scale, down_W, down_qa, down_qb, down_scale, sh_gate_W, sh_up_W, sh_down_W):
            b, s, h = hidden_states.shape
            x = hidden_states.reshape(-1, h)
            T = x.shape[0]
            scores = jax.nn.softmax(x @ gate_weight.T, axis=-1)
            topk_w, topk_idx = jax.lax.top_k(scores, TOPK)
            w_dense = jnp.zeros((T, E), x.dtype).at[jnp.arange(T)[:, None], topk_idx].add(topk_w)
            flat = w_dense[:, inv_mapping]
            scalar = flat.sum(-1)
            soft = jax.nn.softmax(jnp.where(flat == 0, -1000000000.0, flat), axis=-1)

            def expert(muW, gW, gqa, gqb, gs, uW, uqa, uqb, us, dW, dqa, dqb, ds, w):
                xe = x + w @ muW.T
                gate = jax.nn.silu(_fused_linear(xe, gW, gqa, gqb, gs, w))
                up = _fused_linear(xe, uW, uqa, uqb, us, w)
                return _fused_linear(gate * up, dW, dqa, dqb, ds, w)
            outs = jax.vmap(expert, in_axes=(0,) * 13 + (1,))(mask_up_W, gate_W, gate_qa, gate_qb, gate_scale, up_W, up_qa, up_qb, up_scale, down_W, down_qa, down_qb, down_scale, soft)
            y = jnp.einsum('fth,tf->th', outs, scalar).reshape(b, s, h)
            sh = jax.nn.silu(hidden_states @ sh_gate_W.T) * (hidden_states @ sh_up_W.T) @ sh_down_W.T
            return y + sh
        return _moe_forward(hidden_states, gate_weight, inv_mapping, mask_up_W, gate_W, gate_qa, gate_qb, gate_scale, up_W, up_qa, up_qb, up_scale, down_W, down_qa, down_qb, down_scale, sh_gate_W, sh_up_W, sh_down_W)
    x = x + _L0_xattn_ref(_layernorm(x, axis=-1), ctx_2048, L0_xattn_context_lens, L0_xattn_Wq, L0_xattn_bq, L0_xattn_gq, L0_xattn_Wk, L0_xattn_bk, L0_xattn_gk, L0_xattn_Wv, L0_xattn_bv, L0_xattn_Wk_img, L0_xattn_bk_img, L0_xattn_gk_img, L0_xattn_Wv_img, L0_xattn_bv_img, L0_xattn_Wo, L0_xattn_bo)
    x = x + _L0_ffn_ref(_layernorm(x, axis=-1), L0_ffn_gate_weight, L0_ffn_inv_mapping, L0_ffn_mask_up_W, L0_ffn_gate_W, L0_ffn_gate_qa, L0_ffn_gate_qb, L0_ffn_gate_scale, L0_ffn_up_W, L0_ffn_up_qa, L0_ffn_up_qb, L0_ffn_up_scale, L0_ffn_down_W, L0_ffn_down_qa, L0_ffn_down_qb, L0_ffn_down_scale, L0_ffn_sh_gate_W, L0_ffn_sh_up_W, L0_ffn_sh_down_W)
    return x

_drawn_inputs = setup_inputs


def setup_inputs(seed=0):
    import zlib

    import numpy as np

    out = dict(_drawn_inputs(seed))
    spreads = {'L0_xattn_bq': (0.0, 0.8),
     'L0_xattn_gq': (1.0, 0.6),
     'L0_xattn_bk': (0.0, 0.8),
     'L0_xattn_gk': (1.0, 0.6),
     'L0_xattn_bv': (0.0, 0.1),
     'L0_xattn_bk_img': (0.0, 0.8),
     'L0_xattn_gk_img': (1.0, 0.6),
     'L0_xattn_bv_img': (0.0, 0.1),
     'L0_xattn_bo': (0.0, 0.1),
     'L0_ffn_gate_scale': (0.10000000149011612, 0.6),
     'L0_ffn_up_scale': (0.10000000149011612, 0.6),
     'L0_ffn_down_scale': (0.10000000149011612, 0.6)}
    factors = {'L0_xattn_Wk': 3.001,
     'L0_xattn_Wk_img': 3.089,
     'L0_ffn_gate_weight': 8.0,
     'L0_ffn_mask_up_W': 8.0,
     'L0_ffn_gate_W': 8.0,
     'L0_ffn_gate_qa': 8.0,
     'L0_ffn_gate_qb': 8.0,
     'L0_ffn_up_W': 8.0,
     'L0_ffn_up_qa': 8.0,
     'L0_ffn_up_qb': 8.0,
     'L0_ffn_down_W': 8.0,
     'L0_ffn_down_qa': 8.0,
     'L0_ffn_down_qb': 8.0,
     'L0_ffn_sh_gate_W': 2.887,
     'L0_ffn_sh_up_W': 2.846,
     'L0_ffn_sh_down_W': 2.834}
    for name, (base, spread) in spreads.items():
        noise = np.random.default_rng([zlib.crc32(name.encode()), seed]).standard_normal(out[name].shape)
        drawn = base * np.exp(spread * noise) if base else spread * noise
        out[name] = jnp.asarray(drawn.astype(out[name].dtype))
    for name, factor in factors.items():
        out[name] = (out[name] * factor).astype(out[name].dtype)
    return out
```

```python
from contextlib import ExitStack

import numpy as np

import concourse.bass as bass
from concourse import mybir

F32 = mybir.dt.float32
BF16 = mybir.dt.bfloat16
I32 = mybir.dt.int32
ALU = mybir.AluOpType
ACT = mybir.ActivationFunctionType
AX = mybir.AxisListType.X

P = 128
B, SQ, D = 8, 256, 256
HEADS, HD = 16, 16
IMG, CTX = 257, 1601
TXT = CTX - IMG
NT_ALL = -(-CTX // P)
NT_SHORT = 4
SHORT_LEN = NT_SHORT * P - IMG
MIXED = IMG // P
S_ALL = NT_ALL + 1
QT = SQ // P
TOK = B * SQ
NTOK = TOK // P
SPLIT = 6 * HD
EXTRA = P - SPLIT
NEG = -float(2.0 ** 100)
FAR = float(2.0 ** 40)
GRP = 4
EXPERTS, SLOTS, RANK, TOPK = 8, 8, 8, 6
INTER, SHARED = 176, 352
I2 = INTER - P
E_ALL = EXPERTS * SLOTS
CH = 512
NCH = TOK // CH
CT = CH // P
EPS_LN, EPS_RMS = 1e-5, 1e-6
MAGIC = 0x5F3759DF
W1C = 4 * P
WR = E_ALL + EXPERTS
SH_T = [(0, P), (P, P), (2 * P, SHARED - 2 * P)]

SEMAPHORES = (
    "dvc", "acc", "plc", "loaded", "bank6_full", "bank7_full", "bank6_free", "bank7_free", "x_in", "ctx_in",
    "xn_done", "kn_done", "qn_done", "v_done", "k1_done", "k2_done", "k3_done", "r1_done", "r2_done",
    "m_done", "bank5_full", "bank5_free", "st_full", "st_free", "p_used", "o_copied", "att_done", "r_w_in",
    "r_dvc", "r_pe", "r_ac", "r_xn", "r_xT", "r_exp_in", "r_wd", "r_wdT", "r_packed", "r_wT", "r_out", "w_in",
    "wb_in", "e_dvc", "e_plc", "wt_in", "wm_full", "wm_done", "qb_done", "a_full", "aw_done", "g_full",
    "sg_done", "sgs_done", "h_done", "d_full", "dw_done", "y_full", "y_done",
)


class Chain:

    def __init__(self, eng, sem):
        self.eng, self.sem, self.n = eng, sem, 0

    def did(self, ins):
        ins.then_inc(self.sem, 1)
        self.n += 1
        return self.n

    def need(self, n):
        self.eng.wait_ge(self.sem, n)

    def link(self, ins):
        self.need(self.did(ins))


def clear(nc, sems):
    with nc.Block() as block:
        @block.gpsimd
        def _(pool):
            for s in sems:
                pool.sem_clear(s)


def rsqrt(dve, c, y, v, t):
    vi, yi = v.bitcast(I32), y.bitcast(I32)
    c.link(dve.tensor_scalar(yi, vi, 1, None, ALU.logical_shift_right))
    c.link(dve.tensor_scalar(yi, yi, -1.0, float(MAGIC), ALU.mult, ALU.add))
    for _ in range(4):
        c.link(dve.scalar_tensor_tensor(t, v, -0.5, y, ALU.mult, ALU.mult))
        c.link(dve.tensor_tensor(t, t, y, ALU.mult))
        c.link(dve.scalar_tensor_tensor(y, t, 1.5, y, ALU.add, ALU.mult))


def spread(ap, at, n):
    ap = ap.unsqueeze(at)
    shape = list(ap.shape)
    shape[at] = n
    return ap.broadcast_to(shape)


def attention(nc, g, NT, tag):
    S = NT + 1
    chunks = [list(range(c, min(c + 4, NT))) for c in range(0, NT, 4)]
    NC = len(chunks)
    kind = [0 if k < MIXED else 1 if k == MIXED else 2 for k in range(NT)]
    W = NT * P
    bank, x1 = g["bank"], g["x1"]
    with ExitStack() as ctx:
        def sb(n, s, d=F32):
            return ctx.enter_context(nc.sbuf_tensor(f"{n}_{tag}", s, d))
        sems = []

        def sem(n):
            sems.append(g["sems"][n])
            return sems[-1]

        KT = sb("KT", [P, HEADS, W], BF16)
        QX = sb("QX", [P, HEADS, SQ], BF16)
        Vx = sb("Vx", [P, S, HEADS, 2 * HD])
        Kst = sb("Kst", [P, 4 * HEADS, SPLIT], BF16)
        Qst = sb("Qst", [P, QT * HEADS, SPLIT], BF16)
        M6 = sb("M6", [P, QT * HEADS, EXTRA], BF16)
        KV = sb("KV", [P, NT, 2 * D])
        xb = sb("xb", [P, QT, D])
        xn = sb("xn", [P, QT, D])
        xnT = sb("xnT", [P, 2, SQ])
        q = sb("q", [P, QT, D])
        junk = sb("junk", [P, D])
        bn = sb("bn", [P, QT, 6])
        mv = sb("mv", [P, QT, 2])
        ms = sb("ms", [P, QT + NT])
        rs = sb("rs", [P, QT + NT])
        tmp = sb("tmp", [P, QT + NT])
        mx = sb("mx", [P, QT * HEADS, 2])
        mxt = sb("mxt", [P, QT * HEADS, NC])
        PT = sb("PT", [P, 2 if NT == NT_SHORT else 1, GRP, 4, SQ])
        PB = PT.shape[1]
        ctxT = (sb("ctxT", [P, S, 2, P]) if NT == NT_SHORT else
                PT[:].rearrange("p a i k n -> p (a i k n)")[:, 0:S * 2 * P].rearrange("p (s k n) -> p s k n", s=S, k=2))
        Osb = sb("Osb", [P, 2 * SQ])
        rden = sb("rden", [P, 4, GRP])
        att = sb("att", [P, QT, D]) if NT == NT_SHORT else xn
        at1 = sb("at1", [P, QT, GRP, HD])
        at2 = sb("at2", [P, QT, GRP, HD])
        attT = sb("attT", [P, 2, SQ]) if NT == NT_SHORT else xnT
        kz = sb("kz", [P, NT])
        idf, idb = g["idf"], g["idb"]
        dvc, acc, plc = sem("dvc"), sem("acc"), sem("plc")
        loaded = sem("loaded")

        with ExitStack() as sctx:
            krow = KV[:].rearrange("p k n -> p (k n)")[:, 0:W]
            lenf = sctx.enter_context(nc.sbuf_tensor(f"lenf_{tag}", [P, 1], F32))
            flag = sctx.enter_context(nc.sbuf_tensor(f"flag_{tag}", [P, 1], F32))
            with nc.Block() as block:
                @block.sync
                def _(sp):
                    sp.dma_start(krow[SPLIT:P, :], g["key_rows"][:, 0:W]).then_inc(loaded, 16)

                @block.scalar
                def _(act):
                    act.wait_ge(loaded, 16)

                @block.tensor
                def _(pe):
                    pe.wait_ge(loaded, 16)

                @block.gpsimd
                def _(pool):
                    pool.wait_ge(loaded, 16)

                @block.vector
                def _(dve):
                    c = Chain(dve, dvc)
                    c.did(dve.memset(QX[:], 0.0))
                    c.did(dve.memset(M6[:], 0.0))
                    c.did(dve.memset(Vx[:], 0.0))
                    c.link(dve.tensor_copy(lenf[:], g["len"][:]))
                    c.link(dve.tensor_scalar(flag[:], lenf[:], 1.0, None, ALU.is_ge))
                    c.did(dve.memset(M6[:, :, 0:1], 1.0))
                    c.did(dve.memset(QX[SPLIT:SPLIT + 1, :, :], 1.0))
                    for s in range(S):
                        c.did(dve.tensor_scalar(Vx[:, s, :, HD:2 * HD], Vx[:, s, :, HD:2 * HD],
                                                g["vmask"][:, s:s + 1], None, ALU.add))
                    c.did(dve.scalar_tensor_tensor(kz[:], g["is_txt"][:, 0:NT], flag[:, 0:1],
                                                   g["is_img"][:, 0:NT], ALU.mult, ALU.add))
                    dve.wait_ge(loaded, 16)
                    m = krow[SPLIT:SPLIT + 1, :]
                    c.link(dve.tensor_scalar(m, m, lenf[SPLIT:SPLIT + 1, 0:1], NEG, ALU.is_ge, ALU.mult))
                    c.link(dve.tensor_scalar(m, m, flag[SPLIT:SPLIT + 1, 0:1], None, ALU.mult))
                    c.link(dve.tensor_copy(KT[SPLIT:P, :, :], spread(krow[SPLIT:P, :], 1, HEADS)))
            clear(nc, sems)

        full = [sem("bank6_full"), sem("bank7_full")]
        free = [sem("bank6_free"), sem("bank7_free")]
        x_in, ctx_in = sem("x_in"), sem("ctx_in")
        xn_done = sem("xn_done")
        kn_done, qn_done = sem("kn_done"), sem("qn_done")
        v_done = sem("v_done")
        k1_done, k2_done, k3_done = sem("k1_done"), sem("k2_done"), sem("k3_done")
        r1_done, r2_done = sem("r1_done"), sem("r2_done")
        m_done = sem("m_done")
        m5_full, m5_free = sem("bank5_full"), sem("bank5_free")
        st_full, st_free = sem("st_full"), sem("st_free")
        p_used, o_copied = sem("p_used"), sem("o_copied")
        att_done = sem("att_done")

        uses = [("xn",), ("q",)] + [("kv", k) for k in range(NT)]
        for ci in range(NC):
            uses += [("kt", ci, hp) for hp in range(HEADS // 2)]
        uses += [("qt", hq) for hq in range(HEADS // 4)]
        uses += [("max", h, qt, ci) for h in range(HEADS) for qt in range(QT) for ci in range(NC)]
        at = {u: j for j, u in enumerate(uses)}

        def take(eng, u):
            j = at[u]
            if j >= 2:
                eng.wait_ge(free[j % 2], j // 2)
            return bank(6 + j % 2)

        def see(eng, u):
            j = at[u]
            eng.wait_ge(full[j % 2], j // 2 + 1)
            return bank(6 + j % 2)

        def copied(eng, u):
            j = at[u]
            eng.wait_ge(free[j % 2], j // 2 + 1)

        def evac_engine(u):
            return "act" if u[0] in ("kt", "qt") and at[u] % 2 else "dve"
        n_chunk_k = lambda ci: len(chunks[ci])

        with nc.Fori(0, B) as b:
            with nc.Block() as block:
                @block.sync
                def _(sp):
                    sp.dma_start(xb[:], g["x"][bass.ds(b, 1)].rearrange("o (t p) d -> p (o t) d", p=P)).then_inc(x_in, 16)
                    sp.dma_start(ctxT[:, :, :, :], g["ctxT"][bass.ds(b, 1), :, 0:S * 2 * P]
                                 .rearrange("o p (s k n) -> p (o s) k n", s=S, k=2)).then_inc(ctx_in, 16)

                @block.gpsimd
                def _(pool):
                    c = Chain(pool, plc)
                    cp = lambda o, i: pool.tensor_scalar(o, i, 1.0, 0.0, ALU.mult, ALU.add)
                    for k in range(NT):
                        copied(pool, ("kv", k))
                        v = KV[:, k, D:2 * D].rearrange("p (h d) -> p h d", d=HD)
                        for s in ([k] if k < MIXED else [k, k + 1] if k == MIXED else [k + 1]):
                            pool.tensor_scalar(Vx[:, s, :, 0:HD], v, g["vmask"][:, s:s + 1], 0.0,
                                               ALU.mult, ALU.add).then_inc(v_done, 1)
                    for ci in range(-1, NC):
                        n = QT if ci < 0 else len(chunks[ci])
                        st = Qst if ci < 0 else Kst
                        src = (q[:] if ci < 0 else KV[:, chunks[ci][0]:chunks[ci][0] + n, 0:D])
                        rows = st[:, 0:n * HEADS, :].rearrange("p a (j d) -> p a j d", d=HD)
                        src = src.rearrange("p t (h d) -> p t h d", d=HD)
                        where2 = [1, 4] if ci < 0 else [3, 4]
                        where3 = [2] if ci < 0 else [5]
                        pool.wait_ge(r1_done, ci + 2)
                        for j in where2:
                            ins = cp(rows[:, :, j, :].rearrange("p (t h) d -> p t h d", h=HEADS), src)
                        ins.then_inc(k2_done, 1)
                        pool.wait_ge(r2_done, ci + 2)
                        for j in where3:
                            ins = cp(rows[:, :, j, :].rearrange("p (t h) d -> p t h d", h=HEADS), src)
                        ins.then_inc(k3_done, 1)

                @block.scalar
                def _(act):
                    copied(act, ("q",))
                    for i in range(QT):
                        act.activation(junk[:], q[:, i, :], ACT.Square, accum_out=ms[:, i:i + 1]).then_inc(acc, 1)
                        act.wait_ge(acc, i + 1)
                    for k in range(NT):
                        copied(act, ("kv", k))
                        act.activation(junk[:], KV[:, k, 0:D], ACT.Square,
                                       accum_out=ms[:, QT + k:QT + k + 1]).then_inc(acc, 1)
                        act.wait_ge(acc, QT + k + 1)
                    for ci in range(-1, NC):
                        n = QT if ci < 0 else len(chunks[ci])
                        st = Qst if ci < 0 else Kst
                        src = (q[:] if ci < 0 else KV[:, chunks[ci][0]:chunks[ci][0] + n, 0:D])
                        rows = st[:, 0:n * HEADS, :].rearrange("p a (j d) -> p a j d", d=HD)
                        src = src.rearrange("p t (h d) -> p t h d", d=HD)
                        act.wait_ge(qn_done if ci < 0 else kn_done, 1)
                        if ci > 0:
                            see(act, ("kt", ci - 1, HEADS // 2 - 1))
                        for j in ([0, 3, 5] if ci < 0 else [0, 1, 2]):
                            ins = act.activation(rows[:, :, j, :].rearrange("p (t h) d -> p t h d", h=HEADS), src, ACT.Copy)
                        ins.then_inc(k1_done, 1)
                        if ci >= 0:
                            for hp in range(HEADS // 2):
                                u = ("kt", ci, hp)
                                if evac_engine(u) == "act":
                                    src_b = see(act, u).bitcast(BF16)
                                    w = n * P
                                    act.activation(KT[0:SPLIT, 2 * hp:2 * hp + 2, ci * 4 * P:ci * 4 * P + w],
                                                   src_b[0:SPLIT, 0:2 * w].rearrange("p (h n) -> p h n", h=2),
                                                   ACT.Copy).then_inc(free[at[u] % 2], 1)
                    for hq in range(HEADS // 4):
                        u = ("qt", hq)
                        if evac_engine(u) == "act":
                            act.activation(QX[0:SPLIT, 4 * hq:4 * hq + 4, :],
                                           see(act, u).bitcast(BF16)[0:SPLIT, :].rearrange("p (h n) -> p h n", h=4),
                                           ACT.Copy).then_inc(free[at[u] % 2], 1)
                    n = 0
                    for gr in range(HEADS // GRP):
                        for ci in range(NC):
                            unit = gr * NC + ci
                            if unit >= PB:
                                act.wait_ge(p_used, unit - PB + 1)
                            for i in range(GRP):
                                act.wait_ge(st_full, n + 1)
                                w = len(chunks[ci]) * SQ
                                act.activation(PT[:, unit % PB, i, 0:len(chunks[ci]), :].rearrange("p k n -> p (k n)"),
                                               g["pair"](n % 2)[:, 0:w], ACT.Exp).then_inc(st_free, 1)
                                n += 1
                        act.wait_ge(p_used, (gr + 1) * NC)
                        if gr:
                            act.wait_ge(m5_full, 1 + gr)
                        act.activation(Osb[:], bank(4), ACT.Copy).then_inc(o_copied, 1)

                @block.vector
                def _(dve):
                    c = Chain(dve, dvc)
                    dve.wait_ge(x_in, 16)
                    for i in range(QT):
                        c.did(dve.bn_stats(bn[:, i, :], xb[:, i, :]))
                    c.need(c.n)
                    for i in range(QT):
                        c.did(dve.bn_aggr(mv[:, i, :], bn[:, i, :]))
                    c.need(c.n)
                    c.link(dve.tensor_scalar(ms[:, 0:QT], mv[:, :, 1], EPS_LN, None, ALU.add))
                    rsqrt(dve, c, rs[:, 0:QT], ms[:, 0:QT], tmp[:, 0:QT])
                    for i in range(QT):
                        ins = dve.tensor_scalar(xn[:, i, :], xb[:, i, :], mv[:, i, 0:1], rs[:, i:i + 1],
                                                ALU.subtract, ALU.mult)
                    ins.then_inc(xn_done, 1)
                    dve.tensor_copy(xnT[:].rearrange("p k n -> p (k n)"), see(dve, ("xn",))).then_inc(free[0], 1)
                    dve.tensor_tensor(q[:], see(dve, ("q",)).rearrange("p (t n) -> p t n", t=QT),
                                      spread(g["bq"][:], 1, QT), ALU.add).then_inc(free[1], 1)
                    for k in range(NT):
                        dve.tensor_tensor(KV[:, k, :], see(dve, ("kv", k)), g["bkv"][:, kind[k], :],
                                          ALU.add).then_inc(free[at[("kv", k)] % 2], 1)
                    dve.wait_ge(acc, QT + NT)
                    c.link(dve.tensor_scalar(ms[:], ms[:], 1.0 / D, EPS_RMS, ALU.mult, ALU.add))
                    rsqrt(dve, c, rs[:], ms[:], tmp[:])
                    c.did(dve.tensor_scalar(rs[:, 0:QT], rs[:, 0:QT], float(HD) ** -0.5, None, ALU.mult))
                    c.link(dve.tensor_tensor(rs[:, QT:QT + NT], rs[:, QT:QT + NT], kz[:], ALU.mult))
                    for i in range(QT):
                        ins = dve.scalar_tensor_tensor(q[:, i, :], q[:, i, :], rs[:, i:i + 1], g["gq"][:],
                                                       ALU.mult, ALU.mult)
                    ins.then_inc(qn_done, 1)
                    for k in range(NT):
                        ins = dve.scalar_tensor_tensor(KV[:, k, 0:D], KV[:, k, 0:D], rs[:, QT + k:QT + k + 1],
                                                       g["gk"][:, kind[k], :], ALU.mult, ALU.mult)
                    ins.then_inc(kn_done, 1)
                    dve.wait_ge(qn_done, 1)
                    dve.wait_ge(kn_done, 1)
                    for ci in range(-1, NC):
                        n = QT if ci < 0 else len(chunks[ci])
                        st = Qst if ci < 0 else Kst
                        src = (q[:] if ci < 0 else KV[:, chunks[ci][0]:chunks[ci][0] + n, 0:D])
                        rows = st[:, 0:n * HEADS, :].rearrange("p a (j d) -> p a j d", d=HD)
                        src = src.rearrange("p t (h d) -> p t h d", d=HD)
                        part = lambda j: rows[:, :, j, :].rearrange("p (t h) d -> p t h d", h=HEADS)
                        dve.wait_ge(k1_done, ci + 2)
                        dve.tensor_tensor(src, src, part(0), ALU.subtract).then_inc(r1_done, 1)
                        dve.wait_ge(k2_done, ci + 2)
                        dve.wait_ge(r1_done, ci + 2)
                        dve.tensor_tensor(src, src, part(4), ALU.subtract).then_inc(r2_done, 1)
                        if ci >= 0:
                            for hp in range(HEADS // 2):
                                u = ("kt", ci, hp)
                                if evac_engine(u) == "dve":
                                    src_b = see(dve, u).bitcast(BF16)
                                    w = n * P
                                    dve.tensor_copy(KT[0:SPLIT, 2 * hp:2 * hp + 2, ci * 4 * P:ci * 4 * P + w],
                                                    src_b[0:SPLIT, 0:2 * w].rearrange("p (h n) -> p h n", h=2)
                                                    ).then_inc(free[at[u] % 2], 1)
                    for hq in range(HEADS // 4):
                        u = ("qt", hq)
                        if evac_engine(u) == "dve":
                            dve.tensor_copy(QX[0:SPLIT, 4 * hq:4 * hq + 4, :],
                                            see(dve, u).bitcast(BF16)[0:SPLIT, :].rearrange("p (h n) -> p h n", h=4)
                                            ).then_inc(free[at[u] % 2], 1)
                    for h in range(HEADS):
                        for qt in range(QT):
                            for ci in range(NC):
                                s_ = see(dve, ("max", h, qt, ci))
                                col = qt * HEADS + h
                                w = len(chunks[ci]) * P
                                lo = 0
                                if ci == 0:
                                    c.did(dve.tensor_reduce(mx[:, col, 0:1], s_[:, 0:IMG], AX, ALU.max))
                                    lo = IMG
                                dve.tensor_reduce(mxt[:, col, ci:ci + 1], s_[:, lo:w], AX, ALU.max).then_inc(
                                    free[at[("max", h, qt, ci)] % 2], 1)
                    c.need(c.n)
                    for e in range(2):
                        last = max(j for j in range(len(uses)) if j % 2 == e)
                        dve.wait_ge(free[e], last // 2 + 1)
                    c.link(dve.tensor_reduce(mx[:, :, 1:2], mxt[:], AX, ALU.max))
                    c.link(dve.tensor_scalar(mx[:], mx[:], -1.0, None, ALU.mult))
                    for j in range(3):
                        dst = M6[:, :, 1 + j:5 + j:3]
                        ins = dve.tensor_copy(dst, mx[:])
                        c.link(ins) if j < 2 else ins.then_inc(m_done, 1)
                        if j < 2:
                            c.link(dve.tensor_tensor(mx[:], mx[:], dst, ALU.subtract))
                    dve.wait_ge(m5_full, 1)
                    src_b = bank(5).bitcast(BF16)
                    for i in range(GRP):
                        ins = dve.tensor_copy(QX[SPLIT:P, i:HEADS:GRP, :],
                                              src_b[EXTRA * i:EXTRA * (i + 1), :].rearrange("p (a n) -> p a n", a=GRP))
                    ins.then_inc(m5_free, 1)
                    for gr in range(HEADS // GRP):
                        dve.wait_ge(m5_full, 2 + gr)
                        o = bank(5).rearrange("p (i t h d) -> p i t h d", i=2, t=QT, h=GRP)
                        c.link(dve.reciprocal(rden[:].rearrange("p (i t) h -> p i t h", i=2), o[:, :, :, :, HD]))
                        for i, dst in ((0, at1), (1, at2)):
                            r_ = rden[:, QT * i:QT * (i + 1), :]
                            ins = dve.tensor_tensor(dst[:], o[:, i, :, :, 0:HD], spread(r_, 3, HD), ALU.mult)
                        ins.then_inc(m5_free, 1)
                        dve.wait_ge(m5_free, gr + 2)
                        dve.tensor_tensor(att[:, :, gr * GRP * HD:(gr + 1) * GRP * HD]
                                          .rearrange("p t (h d) -> p t h d", d=HD), at1[:], at2[:], ALU.add
                                          ).then_inc(att_done, 1)
                    c.did(dve.tensor_tensor(xb[:], xb[:], spread(g["bo"][:], 1, QT), ALU.add))
                    dve.wait_ge(m5_full, 6)
                    dve.tensor_copy(attT[:].rearrange("p k n -> p (k n)"), bank(5)).then_inc(m5_free, 1)
                    c.need(c.n)
                    dve.wait_ge(m5_full, 7)
                    dve.tensor_tensor(x1[:, bass.ds(b * QT, QT), :], bank(5).rearrange("p (t n) -> p t n", t=QT), xb[:],
                                      ALU.add).then_inc(m5_free, 1)

                @block.tensor
                def _(pe):
                    pe.wait_ge(xn_done, 1)
                    o = take(pe, ("xn",))
                    for k in range(2):
                        for i in range(QT):
                            ins = pe.transpose(o[:, k * SQ + i * P:k * SQ + (i + 1) * P], xn[:, i, k * P:(k + 1) * P], idf[:])
                    ins.then_inc(full[0], 1)
                    copied(pe, ("xn",))
                    o = take(pe, ("q",))
                    for i in range(QT):
                        for k in range(2):
                            ins = pe.matmul(o[:, i * D:(i + 1) * D], xnT[:, k, i * P:(i + 1) * P], g["wq"][:, k, :],
                                            start=(k == 0), stop=(k == 1))
                    ins.then_inc(full[1], 1)
                    pe.wait_ge(ctx_in, 16)
                    for k in range(NT):
                        o = take(pe, ("kv", k))
                        pairs = [(k, 0)] if k < MIXED else [(k, 0), (k + 1, 1)] if k == MIXED else [(k + 1, 1)]
                        todo = [(s, w, kk) for s, w in pairs for kk in range(2)]
                        for n, (s, w, kk) in enumerate(todo):
                            ins = pe.matmul(o, ctxT[:, s, kk, :], g["wkv"][:, w, kk, :],
                                            start=(n == 0), stop=(n == len(todo) - 1))
                        ins.then_inc(full[at[("kv", k)] % 2], 1)
                    for ci in range(NC):
                        pe.wait_ge(k1_done, ci + 2)
                        pe.wait_ge(k2_done, ci + 2)
                        pe.wait_ge(k3_done, ci + 2)
                        n = len(chunks[ci])
                        for hp in range(HEADS // 2):
                            u = ("kt", ci, hp)
                            o = take(pe, u).bitcast(BF16)
                            for i in range(2):
                                for kk in range(n):
                                    ins = pe.transpose(o[0:SPLIT, (i * n + kk) * P:(i * n + kk + 1) * P],
                                                       Kst[:, kk * HEADS + 2 * hp + i, :], idb[:])
                            ins.then_inc(full[at[u] % 2], 1)
                    for hq in range(HEADS // 4):
                        u = ("qt", hq)
                        o = take(pe, u).bitcast(BF16)
                        for i in range(4):
                            for kk in range(QT):
                                ins = pe.transpose(o[0:SPLIT, (i * QT + kk) * P:(i * QT + kk + 1) * P],
                                                   Qst[:, kk * HEADS + 4 * hq + i, :], idb[:])
                        ins.then_inc(full[at[u] % 2], 1)
                    first = at[("max", 0, 0, 0)]
                    for e in range(2):
                        pe.wait_ge(free[e], (first + 1 - e) // 2)
                    for h in range(HEADS):
                        for qt in range(QT):
                            for ci in range(NC):
                                u = ("max", h, qt, ci)
                                w = len(chunks[ci]) * P
                                pe.matmul(take(pe, u)[:, 0:w], QX[0:SPLIT + 1, h, qt * P:(qt + 1) * P],
                                          KT[0:SPLIT + 1, h, ci * 4 * P:ci * 4 * P + w], start=True, stop=True
                                          ).then_inc(full[at[u] % 2], 1)
                    pe.wait_ge(m_done, 1)
                    o = bank(5).bitcast(BF16)
                    for a in range(GRP):
                        for qt in range(QT):
                            ins = pe.transpose(o[:, (a * QT + qt) * P:(a * QT + qt + 1) * P],
                                               M6[:, qt * HEADS + GRP * a:qt * HEADS + GRP * (a + 1), :]
                                               .rearrange("p h e -> p (h e)"), idb[:])
                    ins.then_inc(m5_full, 1)
                    pe.wait_ge(m5_free, 1)
                    pe.wait_ge(v_done, S)
                    n = 0
                    for gr in range(HEADS // GRP):
                        if gr:
                            pe.wait_ge(o_copied, gr)
                        for ci in range(NC):
                            for i in range(GRP):
                                h = gr * GRP + i
                                if n >= 2:
                                    pe.wait_ge(st_free, n - 1)
                                for kk, k in enumerate(chunks[ci]):
                                    ins = pe.matmul(g["pair"](n % 2)[:, kk * SQ:(kk + 1) * SQ],
                                                    KT[:, h, k * P:(k + 1) * P], QX[:, h, :], start=True, stop=True)
                                ins.then_inc(st_full, 1)
                                n += 1
                            pe.wait_ge(st_free, n)
                            for kk, k in enumerate(chunks[ci]):
                                for s in ([k] if k < MIXED else [k, k + 1] if k == MIXED else [k + 1]):
                                    txt = s > MIXED
                                    first, last = s in (0, MIXED + 1), s in (MIXED, S - 1)
                                    for i in range(GRP):
                                        ins = pe.matmul(bank(4)[32 * i:32 * i + 32, SQ * txt:SQ * txt + SQ],
                                                        Vx[:, s, gr * GRP + i, :], PT[:, (gr * NC + ci) % PB, i, kk, :],
                                                        start=first, stop=last)
                            ins.then_inc(p_used, 1)
                        pe.wait_ge(o_copied, gr + 1)
                        pe.wait_ge(m5_free, gr + 1)
                        for i in range(4):
                            ins = pe.transpose(bank(5)[:, i * P:(i + 1) * P], Osb[:, i * P:(i + 1) * P], idf[:])
                        ins.then_inc(m5_full, 1)
                    pe.wait_ge(att_done, HEADS // GRP)
                    pe.wait_ge(m5_free, 5)
                    for k in range(2):
                        for i in range(QT):
                            ins = pe.transpose(bank(5)[:, k * SQ + i * P:k * SQ + (i + 1) * P],
                                               att[:, i, k * P:(k + 1) * P], idf[:])
                    ins.then_inc(m5_full, 1)
                    pe.wait_ge(m5_free, 6)
                    for i in range(QT):
                        for k in range(2):
                            ins = pe.matmul(bank(5)[:, i * D:(i + 1) * D], attT[:, k, i * P:(i + 1) * P], g["wo"][:, k, :],
                                            start=(k == 0), stop=(k == 1))
                    ins.then_inc(m5_full, 1)
            clear(nc, sems)


def routing(nc, g, ctx0):
    bank, x1, xT = g["bank"], g["x1"], g["xT"]
    with ExitStack() as ctx:
        def sb(n, s, d=F32):
            return ctx.enter_context(nc.sbuf_tensor(n, s, d))
        sems = []

        def sem(n):
            sems.append(g["sems"][n])
            return sems[-1]

        bn = sb("r_bn", [P, CT, 6])
        mv = sb("r_mv", [P, CT, 2])
        ms = sb("r_ms", [P, CT])
        rs = sb("r_rs", [P, CT])
        tmp = sb("r_tmp", [P, CT])
        xn = sb("r_xn", [P, CT, D])
        xTc = sb("r_xTc", [P, 2, CH])
        gw = sb("r_gw", [P, 2, E_ALL])
        pick = sb("r_pick", [E_ALL + 2, E_ALL])
        inv = sb("r_inv", [E_ALL + 2, E_ALL], I32)
        sc = sb("r_sc", [P, CT, E_ALL + 2])
        m1 = sb("r_m1", [P, CT, 1])
        s1 = sb("r_s1", [P, CT, 1])
        top = sb("r_top", [P, CT, 8])
        left = sb("r_left", [P, CT, E_ALL + 2])
        wdT = sb("r_wdT", [E_ALL + 2, CH])
        fl = sb("r_fl", [P, CT * EXPERTS, SLOTS])
        fm = sb("r_fm", [P, CT * EXPERTS, SLOTS])
        m8 = sb("r_m8", [P, CT * EXPERTS, 1])
        s8 = sb("r_s8", [P, CT * EXPERTS, 1])
        pk = sb("r_pk", [P, CT, WR])
        wTs = sb("r_wTs", [WR, CH])
        w_in, dvc = sem("r_w_in"), sem("r_dvc")
        with nc.Block() as block:
            @block.sync
            def _(sp):
                sp.dma_start(gw[:], g["gate_wT"]).then_inc(w_in, 16)
                sp.dma_start(inv[:], g["inv"].partition_broadcast(E_ALL + 2)).then_inc(w_in, 16)

            @block.vector
            def _(dve):
                c = Chain(dve, dvc)
                c.did(dve.memset(sc[:], 4.0))
                dve.wait_ge(w_in, 32)
                c.link(dve.tensor_copy(pick[:], inv[:]))
                c.link(dve.tensor_scalar(pick[:], pick[:], g["row"][0:E_ALL + 2, 0:1], None, ALU.is_equal))
        clear(nc, sems)
        pe_s, ac = sem("r_pe"), sem("r_ac")
        xn_d, xT_d, e_in, wd_d = sem("r_xn"), sem("r_xT"), sem("r_exp_in"), sem("r_wd")
        wdT_d, pk_d, wT_d, out_d = sem("r_wdT"), sem("r_packed"), sem("r_wT"), sem("r_out")
        with nc.Fori(0, NCH) as ch:
            with nc.Block() as block:
                @block.vector
                def _(dve):
                    c = Chain(dve, dvc)
                    xin = lambda i: x1[:, bass.ds(ch * CT + i, 1), :].rearrange("p o d -> p (o d)")
                    for i in range(CT):
                        c.did(dve.bn_stats(bn[:, i, :], xin(i)))
                    c.need(c.n)
                    for i in range(CT):
                        c.did(dve.bn_aggr(mv[:, i, :], bn[:, i, :]))
                    c.need(c.n)
                    c.link(dve.tensor_scalar(ms[:], mv[:, :, 1], EPS_LN, None, ALU.add))
                    rsqrt(dve, c, rs[:], ms[:], tmp[:])
                    for i in range(CT):
                        ins = dve.tensor_scalar(xn[:, i, :], xin(i), mv[:, i, 0:1], rs[:, i:i + 1],
                                                ALU.subtract, ALU.mult)
                    ins.then_inc(xn_d, 1)
                    for k in range(2):
                        dve.wait_ge(pe_s, k + 1)
                        dve.tensor_copy(xTc[:, k, :], bank(k)).then_inc(xT_d, 1)
                    dve.wait_ge(pe_s, 3)
                    lg = bank(2)[:, 0:CT * E_ALL].rearrange("p (t e) -> p t e", t=CT)
                    sc_ = sc[:, :, 0:E_ALL]
                    c.link(dve.tensor_reduce(m1[:], lg, AX, ALU.max))
                    dve.tensor_tensor(sc_, lg, m1[:].broadcast_to([P, CT, E_ALL]), ALU.subtract).then_inc(e_in, 1)
                    dve.wait_ge(ac, 1)
                    c.link(dve.tensor_reduce(s1[:], sc_, AX, ALU.add))
                    c.link(dve.reciprocal(s1[:], s1[:]))
                    c.link(dve.tensor_tensor(sc_, sc_, s1[:].broadcast_to([P, CT, E_ALL]), ALU.mult))
                    for i in range(CT):
                        c.did(dve.max(top[:, i, :], sc[:, i, :]))
                    c.need(c.n)
                    for i in range(CT):
                        c.did(dve.match_replace(left[:, i, :], top[:, i, :], sc[:, i, :], 0.0))
                    c.need(c.n)
                    dve.tensor_tensor(left[:], sc[:], left[:], ALU.subtract).then_inc(wd_d, 1)
                    dve.wait_ge(pe_s, 4)
                    dve.tensor_copy(wdT[:], bank(3)[0:E_ALL + 2, :]).then_inc(wdT_d, 1)
                    dve.wait_ge(pe_s, 5)
                    c.link(dve.tensor_copy(fl[:].rearrange("p a k -> p (a k)"), bank(4)[:, 0:CT * E_ALL]))
                    c.link(dve.tensor_scalar(fm[:], fl[:], 0.0, -1e9, ALU.is_equal, ALU.mult))
                    c.link(dve.tensor_tensor(fm[:], fm[:], fl[:], ALU.add))
                    c.link(dve.tensor_reduce(m8[:], fm[:], AX, ALU.max))
                    dve.tensor_tensor(fm[:], fm[:], m8[:].broadcast_to([P, CT * EXPERTS, SLOTS]),
                                      ALU.subtract).then_inc(e_in, 1)
                    c.link(dve.tensor_reduce(pk[:, :, E_ALL:WR].rearrange("p t e -> p t e"),
                                             fl[:].rearrange("p (t e) k -> p t e k", t=CT), AX, ALU.add))
                    dve.wait_ge(ac, 2)
                    c.link(dve.tensor_reduce(s8[:], fm[:], AX, ALU.add))
                    c.link(dve.reciprocal(s8[:], s8[:]))
                    dve.tensor_tensor(pk[:, :, 0:E_ALL].rearrange("p t (e k) -> p t e k", k=SLOTS),
                                      fm[:].rearrange("p (t e) k -> p t e k", t=CT),
                                      s8[:].rearrange("p (t e) o -> p t e o", t=CT).broadcast_to([P, CT, EXPERTS, SLOTS]),
                                      ALU.mult).then_inc(pk_d, 1)
                    dve.wait_ge(pe_s, 6)
                    dve.tensor_copy(wTs[:], bank(5)[0:WR, :]).then_inc(wT_d, 1)

                @block.scalar
                def _(act):
                    act.wait_ge(xT_d, 2)
                    act.activation(xT[:, :, bass.ds(ch * CH, CH)], xTc[:], ACT.Copy)
                    act.wait_ge(e_in, 1)
                    act.activation(sc[:, :, 0:E_ALL], sc[:, :, 0:E_ALL], ACT.Exp).then_inc(ac, 1)
                    act.wait_ge(e_in, 2)
                    act.activation(fm[:], fm[:], ACT.Exp).then_inc(ac, 1)

                @block.tensor
                def _(pe):
                    pe.wait_ge(xn_d, 1)
                    for k in range(2):
                        for i in range(CT):
                            ins = pe.transpose(bank(k)[:, i * P:(i + 1) * P], xn[:, i, k * P:(k + 1) * P], g["idf"][:])
                        ins.then_inc(pe_s, 1)
                    pe.wait_ge(xT_d, 2)
                    for i in range(CT):
                        for k in range(2):
                            ins = pe.matmul(bank(2)[:, i * E_ALL:(i + 1) * E_ALL], xTc[:, k, i * P:(i + 1) * P], gw[:, k, :],
                                            start=(k == 0), stop=(k == 1))
                    ins.then_inc(pe_s, 1)
                    pe.wait_ge(wd_d, 1)
                    for i in range(CT):
                        ins = pe.transpose(bank(3)[0:E_ALL + 2, i * P:(i + 1) * P], left[:, i, :], g["idf"][:])
                    ins.then_inc(pe_s, 1)
                    pe.wait_ge(wdT_d, 1)
                    for i in range(CT):
                        ins = pe.matmul(bank(4)[:, i * E_ALL:(i + 1) * E_ALL], wdT[:, i * P:(i + 1) * P], pick[:],
                                        start=True, stop=True)
                    ins.then_inc(pe_s, 1)
                    pe.wait_ge(pk_d, 1)
                    for i in range(CT):
                        ins = pe.transpose(bank(5)[0:WR, i * P:(i + 1) * P], pk[:, i, :], g["idf"][:])
                    ins.then_inc(pe_s, 1)

                @block.sync
                def _(sp):
                    sp.wait_ge(wT_d, 1)
                    sp.dma_start(g["wT_dram"][:, bass.ds(ch * CH, CH)], wTs[:]).then_inc(out_d, 16)
                    sp.wait_ge(out_d, 16)
            clear(nc, sems)


def experts(nc, g):
    bank, x1, xT = g["bank"], g["x1"], g["xT"]
    with ExitStack() as ctx:
        def sb(n, s, d=F32):
            return ctx.enter_context(nc.sbuf_tensor(n, s, d))
        sems = []

        def sem(n):
            sems.append(g["sems"][n])
            return sems[-1]

        W1 = sb("W1", [P, 2, W1C])
        MU = sb("MU", [P, 2, WR])
        WM = sb("WM", [WR, W1C])
        QB = sb("QB", [P, 3 * P])
        QS = sb("QS", [P, 3 * P])
        DW = sb("DW", [P, 2, D])
        DA = sb("DA", [P, 2, E_ALL])
        DB = sb("DB", [E_ALL, D])
        DS = sb("DS", [E_ALL, D])
        wT = sb("wT", [WR, TOK])
        WB = sb("WB", [P, TOK])
        SB = sb("SB", [P, TOK])
        aw = sb("aw", [P, CH])
        sg = sb("sg", [P, 2, CH])
        hh = sb("hh", [P, 2, CH])
        dw = sb("dw", [E_ALL, CH])
        w_in, wb_in, dvc, plc, wt_in = sem("w_in"), sem("wb_in"), sem("e_dvc"), sem("e_plc"), sem("wt_in")
        wm_full, wm_done, q_done = sem("wm_full"), sem("wm_done"), sem("qb_done")
        a_full, aw_done, g_full = sem("a_full"), sem("aw_done"), sem("g_full")
        sg_done, sgs_done, h_done = sem("sg_done"), sem("sgs_done"), sem("h_done")
        d_full, dw_done, y_full, y_done = sem("d_full"), sem("dw_done"), sem("y_full"), sem("y_done")
        SHW = sb("SHW", [P, 2, 2 * SHARED])
        SHD = sb("SHD", [P, 3, D])
        shh = sb("shh", [P, 3, CH])

        with nc.Block() as block:
            @block.sync
            def _(sp):
                sp.dma_start(SHW[:], g["sh_up_gateT"]).then_inc(w_in, 16)
                sp.dma_start(SHD[:], g["sh_downT"]).then_inc(w_in, 16)
                sp.dma_start(wT[:], g["wT_dram"]).then_inc(wt_in, 16)
                sp.wait_ge(wt_in, 16)

            @block.tensor
            def _(pe):
                pe.wait_ge(w_in, 32)
                for ch in range(NCH):
                    cols = slice(ch * CH, (ch + 1) * CH)
                    for i, (m, w) in enumerate(SH_T):
                        n = 3 * ch + i
                        if n:
                            pe.wait_ge(h_done, n)
                        for j in range(2):
                            for k in range(2):
                                ins = pe.matmul(bank(j)[0:w, :], SHW[:, k, j * SHARED + m:j * SHARED + m + w],
                                                xT[:, k, cols], start=(k == 0), stop=(k == 1))
                        ins.then_inc(g_full, 1)
                    pe.wait_ge(h_done, 3 * ch + 3)
                    if ch:
                        pe.wait_ge(y_done, ch)
                    for i in range(CT):
                        for j, (m, w) in enumerate(SH_T):
                            ins = pe.matmul(bank(2 + i // 2)[:, (i % 2) * D:(i % 2 + 1) * D], shh[0:w, j, i * P:(i + 1) * P],
                                            SHD[0:w, j, :], start=(j == 0), stop=(j == 2))
                    ins.then_inc(y_full, 1)

            @block.scalar
            def _(act):
                for n in range(3 * NCH):
                    w = SH_T[n % 3][1]
                    act.wait_ge(g_full, n + 1)
                    if n:
                        act.wait_ge(h_done, n)
                    act.activation(sg[0:w, 0, :], bank(0)[0:w, :], ACT.Silu).then_inc(sg_done, 1)

            @block.vector
            def _(dve):
                for ch in range(NCH):
                    for i, (m, w) in enumerate(SH_T):
                        n = 3 * ch + i
                        dve.wait_ge(sg_done, n + 1)
                        if ch and i == 0:
                            dve.wait_ge(y_full, ch)
                        dve.tensor_tensor(shh[0:w, i, :], bank(1)[0:w, :], sg[0:w, 0, :], ALU.mult).then_inc(h_done, 1)
                    dve.wait_ge(y_full, ch + 1)
                    xs = x1[:, ch * CT:(ch + 1) * CT, :].rearrange("p t d -> p (t d)")
                    dve.tensor_tensor(xs, xs, g["pair"](1), ALU.add).then_inc(y_done, 1)
        clear(nc, sems)

        with nc.Fori(0, EXPERTS) as f:
            with nc.Block() as block:
                @block.sync
                def _(sp):
                    one = bass.ds(f, 1)
                    for dst, name in ((W1[:], "w1T"), (MU[:], "muP")):
                        sp.dma_start(dst, g[name][one].rearrange("o p k n -> p (o k) n")).then_inc(w_in, 16)
                    sp.dma_start(QB[:], g["qbT"][one].rearrange("o p n -> p (o n)")).then_inc(w_in, 16)
                    sp.dma_start(QS[:], g["up_gate_scale"][one].rearrange("o n -> (o n)").partition_broadcast(P)).then_inc(w_in, 16)
                    for dst, name in ((DW[:], "downT"), (DA[:], "down_qaT")):
                        sp.dma_start(dst, g[name][one].rearrange("o p k n -> p (o k) n")).then_inc(w_in, 16)
                    sp.dma_start(DB[:], g["down_qbT"][one].rearrange("o p n -> p (o n)")).then_inc(w_in, 16)
                    sp.dma_start(DS[:], g["down_scale"][one].rearrange("o n -> (o n)").partition_broadcast(E_ALL)).then_inc(w_in, 16)
                    wk = g["wT_dram"][bass.ds(f * SLOTS, SLOTS), :]
                    for s in range(2):
                        sp.dma_start(WB[s * E_ALL:(s + 1) * E_ALL, :], spread(wk, 1, RANK)).then_inc(wb_in, 16)
                    sp.dma_start(SB[:], g["wT_dram"][bass.ds(f + E_ALL, 1), :].rearrange("o n -> (o n)").partition_broadcast(P)).then_inc(wb_in, 16)

                @block.gpsimd
                def _(pool):
                    pool.wait_ge(w_in, 128)
                    pool.tensor_tensor(QB[:], QB[:], QS[:], ALU.mult).then_inc(q_done, 1)
                    pool.tensor_tensor(DB[:], DB[:], DS[:], ALU.mult).then_inc(q_done, 1)
                    pool.wait_ge(wb_in, 48)
                    for n in range(NCH):
                        cols = slice(n * CH, (n + 1) * CH)
                        for j, w in ((0, P), (1, I2)):
                            pool.wait_ge(sg_done, 2 * n + j + 1)
                            if n + j:
                                pool.wait_ge(sgs_done, 2 * n + j)
                            pool.tensor_tensor(sg[64 * j:64 * j + w, j, :], sg[64 * j:64 * j + w, j, :],
                                               SB[64 * j:64 * j + w, cols], ALU.mult).then_inc(sgs_done, 1)

                @block.tensor
                def _(pe):
                    pe.wait_ge(w_in, 128)
                    for k in range(2):
                        ins = pe.matmul(bank(0)[0:WR, :], MU[:, k, :], W1[:, k, :], start=(k == 0), stop=(k == 1))
                    ins.then_inc(wm_full, 1)
                    pe.wait_ge(wm_done, 1)
                    pe.wait_ge(q_done, 2)
                    for n in range(NCH):
                        cols = slice(n * CH, (n + 1) * CH)
                        x_ = lambda k: xT[:, k, cols]
                        if n:
                            pe.wait_ge(aw_done, n)
                        o = bank(0)
                        for k in range(2):
                            pe.matmul(o, W1[:, k, 3 * P:4 * P], x_(k), start=(k == 0), stop=False)
                        pe.matmul(o, WM[:, 3 * P:4 * P], wT[:, cols], start=False, stop=True).then_inc(a_full, 1)
                        if n:
                            pe.wait_ge(h_done, 2 * n)
                        for i in range(3):
                            o = bank(1 + i)
                            for k in range(2):
                                pe.matmul(o, W1[:, k, i * P:(i + 1) * P], x_(k), start=(k == 0), stop=False)
                            pe.matmul(o, WM[:, i * P:(i + 1) * P], wT[:, cols], start=False, stop=False)
                        pe.wait_ge(aw_done, n + 1)
                        for i in range(3):
                            pe.matmul(bank(1 + i), QB[:, i * P:(i + 1) * P], aw[:], start=False, stop=True
                                      ).then_inc(g_full, 1)
                        pe.wait_ge(h_done, 2 * n + 2)
                        if n:
                            pe.wait_ge(dw_done, n)
                        for j, w in ((0, P), (1, I2)):
                            ins = pe.matmul(bank(4)[0:E_ALL, :], DA[0:w, j, :], hh[0:w, j, :], start=(j == 0), stop=(j == 1))
                        ins.then_inc(d_full, 1)
                        if n:
                            pe.wait_ge(y_done, n)
                        for i in range(CT):
                            o = bank(6 + i // 2)[:, (i % 2) * D:(i % 2 + 1) * D]
                            for j, w in ((0, P), (1, I2)):
                                pe.matmul(o, hh[0:w, j, i * P:(i + 1) * P], DW[0:w, j, :], start=(j == 0 and i % 2 == 0),
                                          stop=False, skip_group_check=True)
                        pe.wait_ge(dw_done, n + 1)
                        for i in range(CT):
                            ins = pe.matmul(bank(6 + i // 2)[:, (i % 2) * D:(i % 2 + 1) * D], dw[:, i * P:(i + 1) * P],
                                            DB[:], start=False, stop=True, skip_group_check=True)
                        ins.then_inc(y_full, 1)

                @block.scalar
                def _(act):
                    for n in range(NCH):
                        act.wait_ge(g_full, 3 * n + 3)
                        if n:
                            act.wait_ge(h_done, 2 * n)
                        act.activation(sg[:, 0, :], bank(1), ACT.Silu).then_inc(sg_done, 1)
                        act.activation(sg[64:64 + I2, 1, :], bank(3)[0:I2, :], ACT.Silu).then_inc(sg_done, 1)

                @block.vector
                def _(dve):
                    dve.wait_ge(wm_full, 1)
                    dve.tensor_copy(WM[:], bank(0)[0:WR, :]).then_inc(wm_done, 1)
                    dve.wait_ge(wb_in, 48)
                    for n in range(NCH):
                        cols = slice(n * CH, (n + 1) * CH)
                        dve.wait_ge(a_full, n + 1)
                        if n:
                            dve.wait_ge(g_full, 3 * n)
                        dve.tensor_tensor(aw[:], bank(0), WB[:, cols], ALU.mult).then_inc(aw_done, 1)
                        dve.wait_ge(sgs_done, 2 * n + 1)
                        if n:
                            dve.wait_ge(y_full, n)
                        dve.tensor_tensor(hh[:, 0, :], bank(2), sg[:, 0, :], ALU.mult).then_inc(h_done, 1)
                        dve.wait_ge(sgs_done, 2 * n + 2)
                        dve.tensor_tensor(hh[0:I2, 1, :], bank(3)[64:64 + I2, :], sg[64:64 + I2, 1, :], ALU.mult
                                          ).then_inc(h_done, 1)
                        dve.wait_ge(d_full, n + 1)
                        dve.tensor_tensor(dw[:], bank(4)[0:E_ALL, :], WB[0:E_ALL, cols], ALU.mult).then_inc(dw_done, 1)
                        dve.wait_ge(y_full, n + 1)
                        xs = x1[:, n * CT:(n + 1) * CT, :].rearrange("p t d -> p (t d)")
                        dve.tensor_tensor(xs, xs, g["pair"](3), ALU.add).then_inc(y_done, 1)
            clear(nc, sems)


def build(nc, a, out):
    g = dict(a)
    with ExitStack() as ctx:
        def sb(n, s, d=F32):
            return ctx.enter_context(nc.sbuf_tensor(n, s, d))
        psum = ctx.enter_context(nc.psum_tensor("psum", [P, 8, 512], F32))
        g["bank"] = lambda n: psum[:, n, :]
        g["pair"] = lambda n: psum[:, 2 * n:2 * n + 2, :].rearrange("p a n -> p (a n)")
        g["wT_dram"] = nc.dram_tensor("wT_dram", (WR, TOK), F32).ap()
        g["sems"] = {n: ctx.enter_context(nc.semaphore(n)) for n in SEMAPHORES}
        g["x1"] = sb("x1", [P, NTOK, D])
        idf, idb, row = sb("idf", [P, P]), sb("idb", [P, P], BF16), sb("row", [P, 1])
        g.update(idf=idf, idb=idb, row=row)
        loaded, cast, stored = [ctx.enter_context(nc.semaphore(n)) for n in ("c_loaded", "c_cast", "stored")]
        with ExitStack() as actx:
            ab = lambda n, s, d=F32: actx.enter_context(nc.sbuf_tensor(n, s, d))
            wq, wkv, wo = ab("wq", [P, 2, D]), ab("wkv", [P, 2, 2, 2 * D]), ab("wo", [P, 2, D])
            bq, gq, bo = ab("bq", [P, D]), ab("gq", [P, D]), ab("bo", [P, D])
            bkv, gk = ab("bkv", [P, 3, 2 * D]), ab("gk", [P, 3, D])
            vmask, is_img, is_txt = ab("vmask", [P, S_ALL]), ab("is_img", [P, NT_ALL]), ab("is_txt", [P, NT_ALL])
            ln, isfew = ab("ln", [P, 1], I32), ab("isfew", [P, 1], I32)
            lf, lg = ab("lf", [P, 1]), ab("lg", [P, 1])
            pairs = [(idf[:], a["ident"]), (row[:], a["row_no"]), (wq[:], a["wqT"]), (wkv[:], a["wkvT"]), (wo[:], a["woT"]),
                     (bq[:], a["bq"].partition_broadcast(P)), (gq[:], a["gq"].partition_broadcast(P)),
                     (bo[:], a["bo"].partition_broadcast(P)), (vmask[:], a["vmask"]), (is_img[:], a["is_img"]),
                     (is_txt[:], a["is_txt"]), (ln[:], a["lens"].partition_broadcast(P))]
            for k, (lo, hi, which) in enumerate(((0, P, 0), (0, P, 1), (0, P, 1))):
                pairs.append((bkv[:, k, :], a["bkv"][which].partition_broadcast(P)))
                pairs.append((gk[:, k, :], a["gk"][which].partition_broadcast(P)))
            with nc.Block() as block:
                @block.sync
                def _(sp):
                    for dst, src in pairs:
                        sp.dma_start(dst, src).then_inc(loaded, 16)
                    sp.wait_ge(loaded, 16 * len(pairs))
                    sp.dma_start(bkv[0:1, 1, :], a["bkv"][0:1]).then_inc(stored, 16)
                    sp.dma_start(gk[0:1, 1, :], a["gk"][0:1]).then_inc(stored, 16)
                    sp.wait_ge(stored, 32)

                @block.vector
                def _(dve):
                    dve.wait_ge(loaded, 16 * len(pairs))
                    c = Chain(dve, cast)
                    c.did(dve.tensor_copy(idb[:], idf[:]))
                    c.link(dve.tensor_copy(lf[:], ln[:]))
                    c.link(dve.tensor_scalar(lg[:], lf[:], 1.0, None, ALU.is_ge))
                    c.link(dve.tensor_scalar(lf[:], lf[:], float(SHORT_LEN), None, ALU.is_le))
                    c.link(dve.tensor_tensor(isfew[:], lf[:], lg[:], ALU.mult))
            clear(nc, [loaded, cast, stored])
            g.update(wq=wq, wkv=wkv, wo=wo, bq=bq, gq=gq, bo=bo, bkv=bkv, gk=gk, vmask=vmask, is_img=is_img,
                     is_txt=is_txt, len=ln)
            few = nc.values_load(isfew[0:1, 0:1], min_val=0, max_val=1)
            with nc.If(few > 0):
                attention(nc, g, NT_SHORT, "few")
            with nc.Else():
                attention(nc, g, NT_ALL, "all")
        with ExitStack() as ectx:
            g["xT"] = ectx.enter_context(nc.sbuf_tensor("xT", [P, 2, TOK], F32))
            routing(nc, g, ctx)
            experts(nc, g)
        with nc.Block() as block:
            @block.sync
            def _(sp):
                sp.dma_start(out.rearrange("b (t p) d -> p (b t) d", p=P), g["x1"][:]).then_inc(stored, 16)
                sp.wait_ge(stored, 16)


def lay_out(i):
    f = lambda n: np.ascontiguousarray(i[n])
    z = lambda *s: np.zeros(s, np.float32)
    halves = lambda w: np.ascontiguousarray(w.reshape(w.shape[:-2] + (w.shape[-2] // P, P, w.shape[-1])).swapaxes(-3, -2))
    o = {"x": f("x")}
    c = f("ctx_2048").transpose(0, 2, 1)
    slots = z(B, D, S_ALL, P)
    for k in range(NT_ALL):
        part = c[:, :, k * P:(k + 1) * P]
        if k == MIXED:
            slots[:, :, k, 0:1] = part[:, :, 0:1]
            slots[:, :, k + 1, 1:] = part[:, :, 1:]
        else:
            slots[:, :, k + (k > MIXED), 0:part.shape[2]] = part
    o["ctxT"] = np.ascontiguousarray(slots.reshape(B, 2, P, S_ALL, P).transpose(0, 2, 3, 1, 4)).reshape(B, P, -1)
    L = "L0_xattn_"
    o["wqT"], o["woT"] = halves(f(L + "Wq")), halves(f(L + "Wo"))
    wkv = np.stack([np.concatenate([f(L + "Wk_img"), f(L + "Wv_img")], 1), np.concatenate([f(L + "Wk"), f(L + "Wv")], 1)])
    o["wkvT"] = np.ascontiguousarray(halves(wkv).transpose(1, 0, 2, 3))
    o["bq"], o["gq"], o["bo"], o["lens"] = f(L + "bq"), f(L + "gq"), f(L + "bo"), f(L + "context_lens")
    o["bkv"] = np.stack([np.concatenate([f(L + "bk_img"), f(L + "bv_img")]), np.concatenate([f(L + "bk"), f(L + "bv")])])
    o["gk"] = np.stack([f(L + "gk_img"), f(L + "gk")])
    tok = np.arange(NT_ALL * P)
    o["ident"] = np.eye(P, dtype=np.float32)
    o["row_no"] = np.arange(P, dtype=np.float32)[:, None]
    rows = z(EXTRA, NT_ALL * P)
    rows[0] = np.where(tok < IMG, -FAR, np.where(tok < CTX, tok - IMG, FAR))
    rows[1:4] = tok < IMG
    rows[4:7] = tok >= IMG
    o["key_rows"] = rows
    o["is_img"] = np.ascontiguousarray((tok < IMG).astype(np.float32).reshape(NT_ALL, P).T)
    o["is_txt"] = np.ascontiguousarray((tok >= IMG).astype(np.float32).reshape(NT_ALL, P).T)
    real = (tok < CTX).astype(np.float32).reshape(NT_ALL, P).T
    vm = np.concatenate([real[:, :MIXED + 1], real[:, MIXED:]], 1)
    vm[:, MIXED], vm[:, MIXED + 1] = o["is_img"][:, MIXED], o["is_txt"][:, MIXED]
    o["vmask"] = np.ascontiguousarray(vm)
    E = "L0_ffn_"
    o["gate_wT"] = halves(f(E + "gate_weight").T)
    o["inv"] = f(E + "inv_mapping").reshape(-1)
    gT, uT = f(E + "gate_W").transpose(0, 2, 1), f(E + "up_W").transpose(0, 2, 1)
    qa = lambda n: f(E + n).reshape(EXPERTS, E_ALL, -1).transpose(0, 2, 1)
    w1 = z(EXPERTS, D, W1C)
    w1[:, :, 0:P], w1[:, :, P:2 * P] = gT[:, :, 0:P], uT[:, :, 0:P]
    w1[:, :, 2 * P:2 * P + I2], w1[:, :, 2 * P + 64:2 * P + 64 + I2] = gT[:, :, P:], uT[:, :, P:]
    w1[:, :, 3 * P:3 * P + 64], w1[:, :, 3 * P + 64:] = qa("gate_qa"), qa("up_qa")
    o["w1T"] = halves(w1)
    mu = z(EXPERTS, D, WR)
    for e in range(EXPERTS):
        mu[e, :, e * SLOTS:(e + 1) * SLOTS] = f(E + "mask_up_W")[e]
    o["muP"] = halves(mu)
    qb = lambda n: f(E + n).transpose(0, 1, 3, 2).reshape(EXPERTS, E_ALL, -1)
    q = z(EXPERTS, P, 3 * P)
    q[:, 0:64, 0:P], q[:, 64:, P:2 * P] = qb("gate_qb")[:, :, 0:P], qb("up_qb")[:, :, 0:P]
    q[:, 0:64, 2 * P:2 * P + I2], q[:, 64:, 2 * P + 64:2 * P + 64 + I2] = qb("gate_qb")[:, :, P:], qb("up_qb")[:, :, P:]
    o["qbT"] = q
    s = z(EXPERTS, 3 * P)
    gs, us = f(E + "gate_scale"), f(E + "up_scale")
    s[:, 0:P], s[:, P:2 * P], s[:, 2 * P:2 * P + I2], s[:, 2 * P + 64:2 * P + 64 + I2] = gs[:, 0:P], us[:, 0:P], gs[:, P:], us[:, P:]
    o["up_gate_scale"] = s

    def pad(w, rows):
        p = z(w.shape[0], rows, w.shape[2])
        p[:, 0:w.shape[1]] = w
        return halves(p)
    o["downT"] = pad(f(E + "down_W").transpose(0, 2, 1), 2 * P)
    o["down_qaT"] = pad(qa("down_qa"), 2 * P)
    o["down_qbT"] = np.ascontiguousarray(qb("down_qb"))
    o["down_scale"] = f(E + "down_scale")
    o["sh_up_gateT"] = halves(np.concatenate([f(E + "sh_gate_W").T, f(E + "sh_up_W").T], 1))
    o["sh_downT"] = pad(f(E + "sh_down_W").T[None], 3 * P)[0]
    return {k: np.ascontiguousarray(v) for k, v in o.items()}


def kernel(**inputs):
    import concourse.bacc as bacc
    from concourse.bass_utils import run_bass_kernel_spmd

    nc = bacc.Bacc("TRN2", target_bir_lowering=False, num_devices=1)
    arrays = {f"in_{k}": v for k, v in lay_out(inputs).items()}
    a = {k[3:]: nc.dram_tensor(k, v.shape, mybir.dt.from_np(v.dtype), kind="ExternalInput").ap() for k, v in arrays.items()}
    out = nc.dram_tensor("out", (B, SQ, D), F32, kind="ExternalOutput").ap()
    build(nc, a, out)
    return run_bass_kernel_spmd(nc, [arrays], core_ids=[0]).results[0]["out"]
```

```python
from contextlib import ExitStack

import numpy as np

import concourse.bass as bass
from concourse import mybir

F32 = mybir.dt.float32
BF16 = mybir.dt.bfloat16
F32R = mybir.dt.float32r
I32 = mybir.dt.int32
ALU = mybir.AluOpType
ACT = mybir.ActivationFunctionType
AX = mybir.AxisListType.X

P = 128
B, SQ, D = 8, 256, 256
HEADS, HD = 16, 16
IMG, CTX = 257, 1601
TXT = CTX - IMG
NT_ALL = -(-CTX // P)
NT_SHORT = 4
SHORT_LEN = NT_SHORT * P - IMG
MIXED = IMG // P
S_ALL = NT_ALL + 1
QT = SQ // P
TOK = B * SQ
NTOK = TOK // P
SPLIT = 6 * HD
EXTRA = P - SPLIT
NEG = -float(2.0 ** 100)
FAR = float(2.0 ** 40)
GRP = 4
EXPERTS, SLOTS, RANK, TOPK = 8, 8, 8, 6
INTER, SHARED = 176, 352
I2 = INTER - P
E_ALL = EXPERTS * SLOTS
CH = 512
NCH = TOK // CH
CT = CH // P
EPS_LN, EPS_RMS = 1e-5, 1e-6
MAGIC = 0x5F3759DF
W1C = 4 * P
TERMS = ((0, 0), (0, 1), (0, 2), (1, 0), (1, 1), (2, 0))
SH_T = [(0, P), (P, P), (2 * P, SHARED - 2 * P)]

SEMAPHORES = (
    "dvc", "acc", "loaded", "ctx_once", "v_zero", "mask_ready", "bank6_full", "bank7_full", "bank6_free", "bank7_free", "ctx_in",
    "xn_done", "kn_done", "qn_done", "max_full", "max_free", "k1_done", "k2_done", "k3_done", "r1_done", "r2_done",
    "m_done", "bank5_full", "bank5_free", "st_full", "st_free", "p_used", "o_copied", "att_done", "r_w_in",
    "r_dvc", "r_pe", "r_ac", "r_xn", "r_xT", "r_exp_in", "r_wd", "r_wdT", "r_packed", "r_wT", "r_out", "w_in_a",
    "w_in_b", "sh_in", "e_dvc", "wm_full", "wm_read", "wm_done", "qb_done", "a_full", "aw_done", "g_full",
    "sg_done", "h_done", "d_full", "dw_done", "y_full", "y_done", "split_done",
)


class Chain:

    def __init__(self, eng, sem):
        self.eng, self.sem, self.n = eng, sem, 0

    def did(self, ins):
        ins.then_inc(self.sem, 1)
        self.n += 1
        return self.n

    def need(self, n):
        self.eng.wait_ge(self.sem, n)

    def link(self, ins):
        self.need(self.did(ins))


def clear(nc, sems):
    with nc.Block() as block:
        @block.gpsimd
        def _(pool):
            for s in sems:
                pool.sem_clear(s)


def rsqrt(dve, c, y, v, t):
    vi, yi = v.bitcast(I32), y.bitcast(I32)
    c.link(dve.tensor_scalar(yi, vi, 1, None, ALU.logical_shift_right))
    c.link(dve.tensor_scalar(yi, yi, -1.0, float(MAGIC), ALU.mult, ALU.add))
    for _ in range(3):
        c.link(dve.scalar_tensor_tensor(t, v, -0.5, y, ALU.mult, ALU.mult))
        c.link(dve.tensor_tensor(t, t, y, ALU.mult))
        c.link(dve.scalar_tensor_tensor(y, t, 1.5, y, ALU.add, ALU.mult))


def spread(ap, at, n):
    ap = ap.unsqueeze(at)
    shape = list(ap.shape)
    shape[at] = n
    return ap.broadcast_to(shape)


def attention(nc, g, NT, tag):
    S = NT + 1
    chunks = [list(range(c, min(c + 4, NT))) for c in range(0, NT, 4)]
    NC = len(chunks)
    kind = [0 if k < MIXED else 1 if k == MIXED else 2 for k in range(NT)]
    W = NT * P
    bank, x1 = g["bank"], g["x1"]
    with ExitStack() as ctx:
        def sb(n, s, d=F32):
            return ctx.enter_context(nc.sbuf_tensor(f"{n}_{tag}", s, d))
        sems = []

        def sem(n):
            sems.append(g["sems"][n])
            return sems[-1]

        PREFETCH = int(NT == NT_SHORT)
        double = lambda n, s, d=F32: [sb(f"{n}_{j}", s, d) for j in range(1 + PREFETCH)]
        KT = double("KT", [P, HEADS, W], BF16)
        QX = double("QX", [P, HEADS, SQ], BF16)
        Vx = double("Vx", [P, S, HEADS, 2 * HD])
        Kst = sb("Kst", [P, 4 * HEADS, SPLIT], BF16)
        Qst = sb("Qst", [P, QT * HEADS, SPLIT], BF16)
        M6 = sb("M6", [P, QT * HEADS, EXTRA], BF16)
        KV = sb("KV", [P, NT, 2 * D])
        xn = sb("xn", [P, QT, D])
        xnT = sb("xnT", [P, 2, SQ])
        q = sb("q", [P, QT, D])
        junk = sb("junk", [P, D])
        ln_b = sb("ln_b", [P, QT, 2])
        ms = sb("ms", [P, QT + NT])
        rs = sb("rs", [P, QT + NT])
        tmp = sb("tmp", [P, QT + NT])
        mx = sb("mx", [P, QT * HEADS, 2])
        mxt = sb("mxt", [P, QT * HEADS, NC])
        PT = sb("PT", [P, 1 + PREFETCH, GRP, 4, SQ])
        PB = PT.shape[1]
        ctxT = (double("ctxT", [P, S, 2, P]) if PREFETCH else
                [PT[:].rearrange("p a i k n -> p (a i k n)")[:, 0:S * 2 * P].rearrange("p (s k n) -> p s k n", s=S, k=2)])
        Osb = sb("Osb", [P, 2 * SQ])
        rden = sb("rden", [P, 4, GRP])
        att = sb("att", [P, QT, D]) if NT == NT_SHORT else xn
        at1 = sb("at1", [P, QT, GRP, HD])
        at2 = sb("at2", [P, QT, GRP, HD])
        attT = sb("attT", [P, 2, SQ]) if NT == NT_SHORT else xnT
        kz = sb("kz", [P, NT])
        idf, idb = g["idf"], g["idb"]
        dvc, acc, loaded, ctx_once = sem("dvc"), sem("acc"), sem("loaded"), sem("ctx_once")
        v_zero, mask_ready = sem("v_zero"), sem("mask_ready")

        with ExitStack() as sctx:
            krow = KV[:].rearrange("p k n -> p (k n)")[:, 0:W]
            lenf = sctx.enter_context(nc.sbuf_tensor(f"lenf_{tag}", [P, 1], F32))
            flag = sctx.enter_context(nc.sbuf_tensor(f"flag_{tag}", [P, 1], F32))
            with nc.Block() as block:
                @block.sync
                def _(sp):
                    sp.dma_start(krow[SPLIT:P, :], g["key_rows"][:, 0:W]).then_inc(loaded, 16)
                    if PREFETCH:
                        sp.dma_start(ctxT[0][:], g["ctxT"][0, :, 0:S * 2 * P].rearrange("p (s k n) -> p s k n", s=S, k=2)
                                     ).then_inc(ctx_once, 16)
                        sp.wait_ge(ctx_once, 16)

                @block.scalar
                def _(act):
                    act.wait_ge(loaded, 16)
                    if PREFETCH:
                        act.wait_ge(mask_ready, 1)
                        act.activation(KT[1][SPLIT:P, :, :], spread(krow[SPLIT:P, :], 1, HEADS), ACT.Copy)

                @block.tensor
                def _(pe):
                    pe.wait_ge(loaded, 16)

                @block.gpsimd
                def _(pool):
                    for t in Vx:
                        ins = pool.memset(t[:], 0.0)
                    ins.then_inc(v_zero, 1)
                    pool.wait_ge(loaded, 16)

                @block.vector
                def _(dve):
                    c = Chain(dve, dvc)
                    c.did(dve.memset(M6[:], 0.0))
                    c.link(dve.tensor_copy(lenf[:], g["len"][:]))
                    c.link(dve.tensor_scalar(flag[:], lenf[:], 1.0, None, ALU.is_ge))
                    c.did(dve.memset(M6[:, :, 0:1], 1.0))
                    for t in QX:
                        c.did(dve.memset(t[SPLIT:SPLIT + 1, :, :], 1.0))
                    dve.wait_ge(v_zero, 1)
                    for t in Vx:
                        for s in range(S):
                            c.did(dve.tensor_scalar(t[:, s, :, HD:2 * HD], t[:, s, :, HD:2 * HD],
                                                    g["vmask"][:, s:s + 1], None, ALU.add))
                    c.did(dve.scalar_tensor_tensor(kz[:], g["is_txt"][:, 0:NT], flag[:, 0:1],
                                                   g["is_img"][:, 0:NT], ALU.mult, ALU.add))
                    dve.wait_ge(loaded, 16)
                    m = krow[SPLIT:SPLIT + 1, :]
                    c.link(dve.tensor_scalar(m, m, lenf[SPLIT:SPLIT + 1, 0:1], NEG, ALU.is_ge, ALU.mult))
                    dve.tensor_scalar(m, m, flag[SPLIT:SPLIT + 1, 0:1], None, ALU.mult).then_inc(mask_ready, 1)
                    dve.wait_ge(mask_ready, 1)
                    dve.tensor_copy(KT[0][SPLIT:P, :, :], spread(krow[SPLIT:P, :], 1, HEADS))
            clear(nc, sems)

        full = [sem("bank6_full"), sem("bank7_full")]
        free = [sem("bank6_free"), sem("bank7_free")]
        ctx_in = sem("ctx_in")
        xn_done = sem("xn_done")
        kn_done, qn_done = sem("kn_done"), sem("qn_done")
        max_full, max_free = sem("max_full"), sem("max_free")
        k1_done, k2_done, k3_done = sem("k1_done"), sem("k2_done"), sem("k3_done")
        r1_done, r2_done = sem("r1_done"), sem("r2_done")
        m_done = sem("m_done")
        m5_full, m5_free = sem("bank5_full"), sem("bank5_free")
        st_full, st_free = sem("st_full"), sem("st_free")
        p_used, o_copied = sem("p_used"), sem("o_copied")
        att_done = sem("att_done")

        uses = [("xn",), ("q",)] + [("kv", k) for k in range(NT)] + [("qt", hq) for hq in range(HEADS // 4)]
        uses += [("kt", ci, hp) for ci in range(NC) for hp in range(HEADS // 2)] + [("mt",)]
        at = {u: j for j, u in enumerate(uses)}

        def take(eng, u):
            j = at[u]
            if j >= 2:
                eng.wait_ge(free[j % 2], j // 2)
            return bank(6 + j % 2)

        def see(eng, u):
            j = at[u]
            eng.wait_ge(full[j % 2], j // 2 + 1)
            return bank(6 + j % 2)

        def copied(eng, u):
            j = at[u]
            eng.wait_ge(free[j % 2], j // 2 + 1)

        def load_keys(sp, b, par):
            sp.dma_start(ctxT[par][:, :, :, :], g["ctxT"][bass.ds(b, 1), :, 0:S * 2 * P]
                         .rearrange("o p (s k n) -> p (o s) k n", s=S, k=2)).then_inc(ctx_in, 16)

        def parts_of(ci):
            n = QT if ci < 0 else len(chunks[ci])
            st = Qst if ci < 0 else Kst
            src = (q[:] if ci < 0 else KV[:, chunks[ci][0]:chunks[ci][0] + n, 0:D]).rearrange("p t (h d) -> p t h d", d=HD)
            rows = st[:, 0:n * HEADS, :].rearrange("p a (j d) -> p a j d", d=HD)
            return n, src, lambda j: rows[:, :, j, :].rearrange("p (t h) d -> p t h d", h=HEADS)

        def step(front=None, back=None, ahead=None):
            if front:
                fb, fp = front
            if back:
                bb, bp = back
            with nc.Block() as block:
                @block.sync
                def _(sp):
                    loads = 0
                    if front and PREFETCH == 0:
                        load_keys(sp, fb, fp)
                        loads += 1
                    if ahead:
                        load_keys(sp, *ahead)
                        loads += 1
                    if loads:
                        sp.wait_ge(ctx_in, 16 * loads)

                @block.gpsimd
                def _(pool):
                    if not front:
                        return
                    cp = lambda o, i: pool.tensor_scalar(o, i, 1.0, 0.0, ALU.mult, ALU.add)
                    for k in range(NT):
                        copied(pool, ("kv", k))
                        v = KV[:, k, D:2 * D].rearrange("p (h d) -> p h d", d=HD)
                        for s in ([k] if k < MIXED else [k, k + 1] if k == MIXED else [k + 1]):
                            pool.tensor_scalar(Vx[fp][:, s, :, 0:HD], v, g["vmask"][:, s:s + 1], 0.0, ALU.mult, ALU.add)
                    for ci in range(-1, NC):
                        n, src, part = parts_of(ci)
                        pool.wait_ge(r1_done, ci + 2)
                        cp(part(4), src).then_inc(k2_done, 1)
                        pool.wait_ge(k2_done, 2 * (ci + 1) + 1)
                        cp(part(1 if ci < 0 else 3), part(4)).then_inc(k2_done, 1)
                        pool.wait_ge(r2_done, ci + 2)
                        cp(part(2 if ci < 0 else 5), src).then_inc(k3_done, 1)

                @block.scalar
                def _(act):
                    def square(i, src):
                        act.activation(junk[:], src, ACT.Square, accum_out=ms[:, i:i + 1]).then_inc(acc, 1)

                    def squares_of_keys(k):
                        copied(act, ("kv", k))
                        act.wait_ge(acc, QT + k)
                        square(QT + k, KV[:, k, 0:D])

                    def squares_of_queries():
                        copied(act, ("q",))
                        for i in range(QT):
                            if i:
                                act.wait_ge(acc, i)
                            square(i, q[:, i, :])

                    def first_parts(ci):
                        n, src, part = parts_of(ci)
                        act.wait_ge(qn_done if ci < 0 else kn_done, 1)
                        if ci > 0:
                            see(act, ("kt", ci - 1, HEADS // 2 - 1))
                        act.activation(part(0), src, ACT.Copy).then_inc(k1_done, 1)
                        act.wait_ge(k1_done, 3 * (ci + 1) + 1)
                        for j in ([3, 5] if ci < 0 else [1, 2]):
                            act.activation(part(j), part(0), ACT.Copy).then_inc(k1_done, 1)

                    def key_rows(ci, hp):
                        w = len(chunks[ci]) * P
                        u = ("kt", ci, hp)
                        act.activation(KT[fp][0:SPLIT, 2 * hp:2 * hp + 2, ci * 4 * P:ci * 4 * P + w],
                                       see(act, u).bitcast(BF16)[0:SPLIT, 0:2 * w].rearrange("p (h n) -> p h n", h=2),
                                       ACT.Copy).then_inc(free[at[u] % 2], 1)

                    def exponentials(n):
                        unit, i = n // GRP, n % GRP
                        ci = unit % NC
                        if i == 0 and unit >= PB:
                            act.wait_ge(p_used, unit - PB + 1)
                        act.wait_ge(st_full, n + 1)
                        w = len(chunks[ci]) * SQ
                        act.activation(PT[:, unit % PB, i, 0:len(chunks[ci]), :].rearrange("p k n -> p (k n)"),
                                       g["pair"](n % 2)[:, 0:w], ACT.Exp).then_inc(st_free, 1)

                    def copy_sums(gr):
                        act.wait_ge(p_used, (gr + 1) * NC)
                        if gr:
                            act.wait_ge(m5_full, gr)
                        act.activation(Osb[:], bank(4), ACT.Copy).then_inc(o_copied, 1)

                    def exponential_units(lo, hi):
                        for n in range(lo * NC, hi * NC):
                            exponentials(n)
                            if n % (GRP * NC) == 1 and n > GRP * NC:
                                copy_sums(n // (GRP * NC) - 1)

                    if back:
                        exponential_units(0, 4)
                    if front:
                        squares_of_queries()
                    if back:
                        exponential_units(4, 6)
                    if front:
                        for k in range(NT):
                            squares_of_keys(k)
                            if back and k == 1:
                                exponential_units(6, 8)
                    if back:
                        exponential_units(8 if front else 6, 10)
                    if front:
                        first_parts(-1)
                    if back:
                        exponential_units(10, 12)
                    if front:
                        first_parts(0)
                    if back:
                        exponential_units(12, 16)
                        copy_sums(3)
                    if front:
                        for ci in range(NC):
                            if ci:
                                first_parts(ci)
                            for hp in range(HEADS // 2):
                                key_rows(ci, hp)
                        o = see(act, ("mt",)).bitcast(BF16)
                        for i in range(2):
                            act.activation(QX[fp][SPLIT:P, i:HEADS:GRP, :],
                                           o[EXTRA * i:EXTRA * (i + 1), :].rearrange("p (a n) -> p a n", a=GRP), ACT.Copy)

                @block.vector
                def _(dve):
                    c = Chain(dve, dvc)

                    def norm_queries():
                        c.link(dve.tensor_copy(ln_b[:], g["x_norm"][:, bass.ds(fb * QT, QT), :]))
                        for i in range(QT):
                            ins = dve.tensor_scalar(xn[:, i, :], x1[:, bass.ds(fb * QT + i, 1), :].rearrange("p o d -> p (o d)"),
                                                    ln_b[:, i, 0:1], ln_b[:, i, 1:2], ALU.subtract, ALU.mult)
                        ins.then_inc(xn_done, 1)

                    def biases():
                        dve.tensor_copy(xnT[:].rearrange("p k n -> p (k n)"), see(dve, ("xn",))
                                        ).then_inc(free[at[("xn",)] % 2], 1)
                        dve.tensor_tensor(q[:], see(dve, ("q",)).rearrange("p (t n) -> p t n", t=QT),
                                          spread(g["bq"][:], 1, QT), ALU.add).then_inc(free[at[("q",)] % 2], 1)
                        for k in range(NT):
                            dve.tensor_tensor(KV[:, k, :], see(dve, ("kv", k)), g["bkv"][:, kind[k], :],
                                              ALU.add).then_inc(free[at[("kv", k)] % 2], 1)

                    def rms_norm():
                        dve.wait_ge(acc, QT + NT)
                        c.link(dve.tensor_scalar(ms[:], ms[:], 1.0 / D, EPS_RMS, ALU.mult, ALU.add))
                        rsqrt(dve, c, rs[:], ms[:], tmp[:])
                        c.did(dve.tensor_scalar(rs[:, 0:QT], rs[:, 0:QT], float(HD) ** -0.5, None, ALU.mult))
                        c.link(dve.tensor_tensor(rs[:, QT:QT + NT], rs[:, QT:QT + NT], kz[:], ALU.mult))
                        for i in range(QT):
                            ins = dve.scalar_tensor_tensor(q[:, i, :], q[:, i, :], rs[:, i:i + 1], g["gq"][:],
                                                           ALU.mult, ALU.mult)
                        ins.then_inc(qn_done, 1)
                        for k in range(NT):
                            ins = dve.scalar_tensor_tensor(KV[:, k, 0:D], KV[:, k, 0:D], rs[:, QT + k:QT + k + 1],
                                                           g["gk"][:, kind[k], :], ALU.mult, ALU.mult)
                        ins.then_inc(kn_done, 1)

                    def first_rest(ci):
                        n, src, part = parts_of(ci)
                        dve.wait_ge(qn_done if ci < 0 else kn_done, 1)
                        dve.wait_ge(k1_done, 3 * (ci + 1) + 1)
                        dve.tensor_tensor(src, src, part(0), ALU.subtract).then_inc(r1_done, 1)

                    def second_rest(ci):
                        n, src, part = parts_of(ci)
                        dve.wait_ge(k2_done, 2 * (ci + 1) + 1)
                        dve.wait_ge(r1_done, ci + 2)
                        dve.tensor_tensor(src, src, part(4), ALU.subtract).then_inc(r2_done, 1)

                    def query_rows(hq):
                        u = ("qt", hq)
                        dve.tensor_copy(QX[fp][0:SPLIT, 4 * hq:4 * hq + 4, :],
                                        see(dve, u).bitcast(BF16)[0:SPLIT, :].rearrange("p (h n) -> p h n", h=4)
                                        ).then_inc(free[at[u] % 2], 1)

                    def maxima(ci, hp):
                        w = len(chunks[ci]) * P
                        for h in (2 * hp, 2 * hp + 1):
                            n = ci * HEADS + h
                            dve.wait_ge(max_full, n + 1)
                            s_ = g["pair"](n % 2).rearrange("p (t n) -> p t n", t=QT)
                            lo = 0
                            if ci == 0:
                                c.did(dve.tensor_reduce(mx[:, h:QT * HEADS:HEADS, 0:1], s_[:, :, 0:IMG], AX, ALU.max))
                                lo = IMG
                            dve.tensor_reduce(mxt[:, h:QT * HEADS:HEADS, ci:ci + 1], s_[:, :, lo:w], AX, ALU.max
                                              ).then_inc(max_free, 1)

                    def minus_maxima():
                        c.need(c.n)
                        dve.wait_ge(max_free, NC * HEADS)
                        c.link(dve.tensor_reduce(mx[:, :, 1:2], mxt[:], AX, ALU.max))
                        c.link(dve.tensor_scalar(mx[:], mx[:], -1.0, None, ALU.mult))
                        for j in range(3):
                            dst = M6[:, :, 1 + j:5 + j:3]
                            ins = dve.tensor_copy(dst, mx[:])
                            c.link(ins) if j < 2 else ins.then_inc(m_done, 1)
                            if j < 2:
                                c.link(dve.tensor_tensor(mx[:], mx[:], dst, ALU.subtract))
                        o = see(dve, ("mt",)).bitcast(BF16)
                        for i in range(2, GRP):
                            ins = dve.tensor_copy(QX[fp][SPLIT:P, i:HEADS:GRP, :],
                                                  o[EXTRA * i:EXTRA * (i + 1), :].rearrange("p (a n) -> p a n", a=GRP))
                        ins.then_inc(free[at[("mt",)] % 2], 1)

                    def divide(gr):
                        dve.wait_ge(m5_full, 1 + gr)
                        o = bank(5).rearrange("p (i t h d) -> p i t h d", i=2, t=QT, h=GRP)
                        c.link(dve.reciprocal(rden[:].rearrange("p (i t) h -> p i t h", i=2), o[:, :, :, :, HD]))
                        for i, dst in ((0, at1), (1, at2)):
                            ins = dve.tensor_tensor(dst[:], o[:, i, :, :, 0:HD], spread(rden[:, QT * i:QT * (i + 1), :], 3, HD),
                                                    ALU.mult)
                        ins.then_inc(m5_free, 1)
                        dve.wait_ge(m5_free, gr + 1)
                        dve.tensor_tensor(att[:, :, gr * GRP * HD:(gr + 1) * GRP * HD]
                                          .rearrange("p t (h d) -> p t h d", d=HD), at1[:], at2[:], ALU.add
                                          ).then_inc(att_done, 1)

                    def output_rows():
                        xs = x1[:, bass.ds(bb * QT, QT), :]
                        c.did(dve.tensor_tensor(xs, xs, spread(g["bo"][:], 1, QT), ALU.add))
                        dve.wait_ge(m5_full, 5)
                        dve.tensor_copy(attT[:].rearrange("p k n -> p (k n)"), bank(5)).then_inc(m5_free, 1)
                        c.need(c.n)

                    def output():
                        xs = x1[:, bass.ds(bb * QT, QT), :]
                        dve.wait_ge(m5_full, 6)
                        dve.tensor_tensor(xs, bank(5).rearrange("p (t n) -> p t n", t=QT), xs, ALU.add).then_inc(m5_free, 1)

                    if front:
                        norm_queries()
                        biases()
                    if back:
                        divide(0)
                    if front:
                        rms_norm()
                        first_rest(-1)
                    if back:
                        divide(1)
                    if front:
                        second_rest(-1)
                        first_rest(0)
                        for hq in range(HEADS // 4):
                            query_rows(hq)
                            if hq == 0:
                                second_rest(0)
                    if back:
                        divide(2)
                    for ci in range(NC if front else 0):
                        if ci:
                            first_rest(ci)
                            second_rest(ci)
                        for hp in range(HEADS // 2):
                            maxima(ci, hp)
                            if back and hp == 2:
                                divide(3)
                            if back and hp == 5:
                                output_rows()
                            if back and hp == 7:
                                output()
                    if front:
                        minus_maxima()
                    elif back:
                        divide(3)
                        output_rows()
                        output()

                @block.tensor
                def _(pe):
                    def project_keys(k):
                        o = take(pe, ("kv", k))
                        todo = [(s, w, kk) for s, w in ([(k, 0)] if k < MIXED else [(k, 0), (k + 1, 1)] if k == MIXED else
                                                        [(k + 1, 1)]) for kk in range(2)]
                        for n, (s, w, kk) in enumerate(todo):
                            ins = pe.matmul(o, ctxT[fp][:, s, kk, :], g["wkv"][:, w, kk, :],
                                            start=(n == 0), stop=(n == len(todo) - 1))
                        ins.then_inc(full[at[("kv", k)] % 2], 1)

                    def query_columns():
                        pe.wait_ge(xn_done, 1)
                        o = take(pe, ("xn",))
                        for k in range(2):
                            for i in range(QT):
                                ins = pe.transpose(o[:, k * SQ + i * P:k * SQ + (i + 1) * P], xn[:, i, k * P:(k + 1) * P], idf[:])
                        ins.then_inc(full[at[("xn",)] % 2], 1)

                    def project_queries():
                        o = take(pe, ("q",))
                        copied(pe, ("xn",))
                        for i in range(QT):
                            for k in range(2):
                                ins = pe.matmul(o[:, i * D:(i + 1) * D], xnT[:, k, i * P:(i + 1) * P], g["wq"][:, k, :],
                                                start=(k == 0), stop=(k == 1))
                        ins.then_inc(full[at[("q",)] % 2], 1)

                    def three_parts(ci):
                        pe.wait_ge(k1_done, 3 * (ci + 2))
                        pe.wait_ge(k2_done, 2 * (ci + 2))
                        pe.wait_ge(k3_done, ci + 2)

                    def query_rows(hq):
                        u = ("qt", hq)
                        o = take(pe, u).bitcast(BF16)
                        for i in range(4):
                            for kk in range(QT):
                                ins = pe.transpose(o[0:SPLIT, (i * QT + kk) * P:(i * QT + kk + 1) * P],
                                                   Qst[:, kk * HEADS + 4 * hq + i, :], idb[:])
                        ins.then_inc(full[at[u] % 2], 1)

                    def key_rows(ci, hp):
                        n = len(chunks[ci])
                        u = ("kt", ci, hp)
                        o = take(pe, u).bitcast(BF16)
                        for i in range(2):
                            for kk in range(n):
                                ins = pe.transpose(o[0:SPLIT, (i * n + kk) * P:(i * n + kk + 1) * P],
                                                   Kst[:, kk * HEADS + 2 * hp + i, :], idb[:])
                        ins.then_inc(full[at[u] % 2], 1)

                    def maxima(ci, hp):
                        copied(pe, ("kt", ci, hp))
                        w = len(chunks[ci]) * P
                        for h in (2 * hp, 2 * hp + 1):
                            n = ci * HEADS + h
                            if n >= 2:
                                pe.wait_ge(max_free, n - 1)
                            for qt in range(QT):
                                ins = pe.matmul(g["pair"](n % 2)[:, qt * 2 * SQ:qt * 2 * SQ + w],
                                                QX[fp][0:SPLIT + 1, h, qt * P:(qt + 1) * P],
                                                KT[fp][0:SPLIT + 1, h, ci * 4 * P:ci * 4 * P + w], start=True, stop=True)
                            ins.then_inc(max_full, 1)

                    def maxima_rows():
                        pe.wait_ge(m_done, 1)
                        o = take(pe, ("mt",)).bitcast(BF16)
                        for a in range(GRP):
                            for qt in range(QT):
                                ins = pe.transpose(o[:, (a * QT + qt) * P:(a * QT + qt + 1) * P],
                                                   M6[:, qt * HEADS + GRP * a:qt * HEADS + GRP * (a + 1), :]
                                                   .rearrange("p h e -> p (h e)"), idb[:])
                        ins.then_inc(full[at[("mt",)] % 2], 1)

                    def scores(n):
                        unit, i = n // GRP, n % GRP
                        h = unit // NC * GRP + i
                        if n >= 2:
                            pe.wait_ge(st_free, n - 1)
                        for kk, k in enumerate(chunks[unit % NC]):
                            ins = pe.matmul(g["pair"](n % 2)[:, kk * SQ:(kk + 1) * SQ],
                                            KT[bp][:, h, k * P:(k + 1) * P], QX[bp][:, h, :], start=True, stop=True)
                        ins.then_inc(st_full, 1)

                    def values(unit):
                        gr, ci = unit // NC, unit % NC
                        if gr and ci == 0:
                            pe.wait_ge(o_copied, gr)
                        pe.wait_ge(st_free, (unit + 1) * GRP)
                        for kk, k in enumerate(chunks[ci]):
                            for s in ([k] if k < MIXED else [k, k + 1] if k == MIXED else [k + 1]):
                                txt = s > MIXED
                                first, last = s in (0, MIXED + 1), s in (MIXED, S - 1)
                                for i in range(GRP):
                                    ins = pe.matmul(bank(4)[32 * i:32 * i + 32, SQ * txt:SQ * txt + SQ],
                                                    Vx[bp][:, s, gr * GRP + i, :], PT[:, unit % PB, i, kk, :],
                                                    start=first, stop=last)
                        ins.then_inc(p_used, 1)

                    def sums_to_tokens(gr):
                        pe.wait_ge(o_copied, gr + 1)
                        if gr:
                            pe.wait_ge(m5_free, gr)
                        for i in range(4):
                            ins = pe.transpose(bank(5)[:, i * P:(i + 1) * P], Osb[:, i * P:(i + 1) * P], idf[:])
                        ins.then_inc(m5_full, 1)

                    def score_units(lo, hi):
                        for n in range(lo * NC, hi * NC):
                            scores(n)
                            if n % GRP == 1 and n > GRP:
                                values(n // GRP - 1)
                            if n % (GRP * NC) == 3 and n > GRP * NC:
                                sums_to_tokens(n // (GRP * NC) - 1)

                    def output_rows():
                        pe.wait_ge(att_done, HEADS // GRP)
                        pe.wait_ge(m5_free, 4)
                        for k in range(2):
                            for i in range(QT):
                                ins = pe.transpose(bank(5)[:, k * SQ + i * P:k * SQ + (i + 1) * P],
                                                   att[:, i, k * P:(k + 1) * P], idf[:])
                        ins.then_inc(m5_full, 1)

                    def output():
                        pe.wait_ge(m5_free, 5)
                        for i in range(QT):
                            for k in range(2):
                                ins = pe.matmul(bank(5)[:, i * D:(i + 1) * D], attT[:, k, i * P:(i + 1) * P], g["wo"][:, k, :],
                                                start=(k == 0), stop=(k == 1))
                        ins.then_inc(m5_full, 1)

                    if front:
                        if PREFETCH == 0:
                            pe.wait_ge(ctx_in, 16)
                    if back:
                        score_units(0, 2)
                    if front:
                        query_columns()
                    if back:
                        score_units(2, 4)
                    if front:
                        project_queries()
                        project_keys(0)
                    if back:
                        score_units(4, 6)
                    if front:
                        project_keys(1)
                        project_keys(2)
                    if back:
                        score_units(6, 8)
                    if front:
                        for k in range(3, NT):
                            project_keys(k)
                    if back:
                        score_units(8, 12)
                    if front:
                        three_parts(-1)
                        for hq in range(2):
                            query_rows(hq)
                    if back:
                        score_units(12, 14)
                    if front:
                        for hq in range(2, HEADS // 4):
                            query_rows(hq)
                    if back:
                        score_units(14, 16)
                        values(HEADS // GRP * NC - 1)
                    for ci in range(NC if front else 0):
                        three_parts(ci)
                        for hp in range(HEADS // 2 + 1):
                            if hp < HEADS // 2:
                                key_rows(ci, hp)
                            if back and hp == 0:
                                sums_to_tokens(3)
                            if hp == 1 and ci == 0:
                                copied(pe, ("qt", 2))
                                copied(pe, ("qt", 3))
                            if hp:
                                maxima(ci, hp - 1)
                            if back and hp == 5:
                                output_rows()
                            if back and hp == 7:
                                output()
                    if front:
                        maxima_rows()
                    elif back:
                        sums_to_tokens(3)
                        output_rows()
                        output()

        if PREFETCH:
            step(front=(0, 0), ahead=(1, 1))
            clear(nc, sems)
            with nc.Fori(0, B // 2 - 1) as pair:
                b = pair * 2
                step(front=(b + 1, 1), back=(b, 0), ahead=(b + 2, 0))
                clear(nc, sems)
                step(front=(b + 2, 0), back=(b + 1, 1), ahead=(b + 3, 1))
                clear(nc, sems)
            step(front=(B - 1, 1), back=(B - 2, 0))
            clear(nc, sems)
            step(back=(B - 1, 1))
            clear(nc, sems)
        else:
            with nc.Fori(0, B) as b:
                step(front=(b, 0))
                clear(nc, sems)
                step(back=(b, 0))
                clear(nc, sems)


def routing(nc, g, ctx0):
    bank, x1, xT = g["bank"], g["x1"], g["xT"]
    with ExitStack() as ctx:
        def sb(n, s, d=F32):
            return ctx.enter_context(nc.sbuf_tensor(n, s, d))
        sems = []

        def sem(n):
            sems.append(g["sems"][n])
            return sems[-1]

        bn = sb("r_bn", [P, CT, 6])
        mv = sb("r_mv", [P, CT, 2])
        ms = sb("r_ms", [P, CT])
        rs = sb("r_rs", [P, CT])
        tmp = sb("r_tmp", [P, CT])
        xn = sb("r_xn", [P, CT, D])
        xTc = sb("r_xTc", [P, 2, CH])
        gw = sb("r_gw", [P, 2, E_ALL])
        pick = sb("r_pick", [E_ALL + 2, E_ALL])
        inv = sb("r_inv", [E_ALL + 2, E_ALL], I32)
        sc = sb("r_sc", [P, CT, E_ALL + 2])
        m1 = sb("r_m1", [P, CT, 1])
        s1 = sb("r_s1", [P, CT, 1])
        top = sb("r_top", [P, CT, 8])
        left = sb("r_left", [P, CT, E_ALL + 2])
        wdT = sb("r_wdT", [E_ALL + 2, CH])
        fl = sb("r_fl", [P, CT * EXPERTS, SLOTS])
        fm = sb("r_fm", [P, CT * EXPERTS, SLOTS])
        m8 = sb("r_m8", [P, CT * EXPERTS, 1])
        s8 = sb("r_s8", [P, CT * EXPERTS, 1])
        pk = sb("r_pk", [P, CT, E_ALL])
        wTs = sb("r_wTs", [E_ALL, CH])
        left_w = sb("r_left_w", [E_ALL, CH])
        parts = sb("r_parts", [E_ALL, 3, CH], BF16)
        w_in, dvc = sem("r_w_in"), sem("r_dvc")
        with nc.Block() as block:
            @block.sync
            def _(sp):
                sp.dma_start(gw[:], g["gate_wT"]).then_inc(w_in, 16)
                sp.dma_start(inv[:], g["inv"].partition_broadcast(E_ALL + 2)).then_inc(w_in, 16)

            @block.vector
            def _(dve):
                c = Chain(dve, dvc)
                c.did(dve.memset(sc[:], 4.0))
                dve.wait_ge(w_in, 32)
                c.link(dve.tensor_copy(pick[:], inv[:]))
                c.link(dve.tensor_scalar(pick[:], pick[:], g["row"][0:E_ALL + 2, 0:1], None, ALU.is_equal))
        clear(nc, sems)
        pe_s, ac = sem("r_pe"), sem("r_ac")
        xn_d, xT_d, e_in, wd_d = sem("r_xn"), sem("r_xT"), sem("r_exp_in"), sem("r_wd")
        wdT_d, pk_d, wT_d, out_d = sem("r_wdT"), sem("r_packed"), sem("r_wT"), sem("r_out")
        with nc.Fori(0, NCH) as ch:
            with nc.Block() as block:
                @block.vector
                def _(dve):
                    c = Chain(dve, dvc)
                    xin = lambda i: x1[:, bass.ds(ch * CT + i, 1), :].rearrange("p o d -> p (o d)")
                    for i in range(CT):
                        c.did(dve.bn_stats(bn[:, i, :], xin(i)))
                    c.need(c.n)
                    for i in range(CT):
                        c.did(dve.bn_aggr(mv[:, i, :], bn[:, i, :]))
                    c.need(c.n)
                    c.link(dve.tensor_scalar(ms[:], mv[:, :, 1], EPS_LN, None, ALU.add))
                    rsqrt(dve, c, rs[:], ms[:], tmp[:])
                    for i in range(CT):
                        ins = dve.tensor_scalar(xn[:, i, :], xin(i), mv[:, i, 0:1], rs[:, i:i + 1],
                                                ALU.subtract, ALU.mult)
                    ins.then_inc(xn_d, 1)
                    for k in range(2):
                        dve.wait_ge(pe_s, k + 1)
                        dve.tensor_copy(xTc[:, k, :], bank(k)).then_inc(xT_d, 1)
                    dve.wait_ge(pe_s, 3)
                    lg = bank(2)[:, 0:CT * E_ALL].rearrange("p (t e) -> p t e", t=CT)
                    sc_ = sc[:, :, 0:E_ALL]
                    c.link(dve.tensor_reduce(m1[:], lg, AX, ALU.max))
                    dve.tensor_tensor(sc_, lg, m1[:].broadcast_to([P, CT, E_ALL]), ALU.subtract).then_inc(e_in, 1)
                    dve.wait_ge(ac, 1)
                    c.link(dve.tensor_reduce(s1[:], sc_, AX, ALU.add))
                    c.link(dve.reciprocal(s1[:], s1[:]))
                    c.link(dve.tensor_tensor(sc_, sc_, s1[:].broadcast_to([P, CT, E_ALL]), ALU.mult))
                    for i in range(CT):
                        c.did(dve.max(top[:, i, :], sc[:, i, :]))
                    c.need(c.n)
                    for i in range(CT):
                        c.did(dve.match_replace(left[:, i, :], top[:, i, :], sc[:, i, :], 0.0))
                    c.need(c.n)
                    dve.tensor_tensor(left[:], sc[:], left[:], ALU.subtract).then_inc(wd_d, 1)
                    dve.wait_ge(pe_s, 4)
                    dve.tensor_copy(wdT[:], bank(3)[0:E_ALL + 2, :]).then_inc(wdT_d, 1)
                    dve.wait_ge(pe_s, 5)
                    c.link(dve.tensor_copy(fl[:].rearrange("p a k -> p (a k)"), bank(4)[:, 0:CT * E_ALL]))
                    c.link(dve.tensor_scalar(fm[:], fl[:], 0.0, -1e9, ALU.is_equal, ALU.mult))
                    c.link(dve.tensor_tensor(fm[:], fm[:], fl[:], ALU.add))
                    c.link(dve.tensor_reduce(m8[:], fm[:], AX, ALU.max))
                    dve.tensor_tensor(fm[:], fm[:], m8[:].broadcast_to([P, CT * EXPERTS, SLOTS]),
                                      ALU.subtract).then_inc(e_in, 1)
                    c.link(dve.tensor_reduce(g["sums"][:, bass.ds(ch * CT, CT), :],
                                             fl[:].rearrange("p (t e) k -> p t e k", t=CT), AX, ALU.add))
                    dve.wait_ge(ac, 2)
                    c.link(dve.tensor_reduce(s8[:], fm[:], AX, ALU.add))
                    c.link(dve.reciprocal(s8[:], s8[:]))
                    dve.tensor_tensor(pk[:].rearrange("p t (e k) -> p t e k", k=SLOTS),
                                      fm[:].rearrange("p (t e) k -> p t e k", t=CT),
                                      s8[:].rearrange("p (t e) o -> p t e o", t=CT).broadcast_to([P, CT, EXPERTS, SLOTS]),
                                      ALU.mult).then_inc(pk_d, 1)
                    dve.wait_ge(pe_s, 6)
                    dve.tensor_copy(wTs[:], bank(5)[0:E_ALL, :]).then_inc(wT_d, 1)
                    dve.wait_ge(wT_d, 1)
                    c.link(dve.tensor_copy(parts[:, 0, :], wTs[:]))
                    c.link(dve.tensor_tensor(left_w[:], wTs[:], parts[:, 0, :], ALU.subtract))
                    c.link(dve.tensor_copy(parts[:, 1, :], left_w[:]))
                    dve.tensor_tensor(parts[:, 2, :], left_w[:], parts[:, 1, :], ALU.subtract).then_inc(wT_d, 1)

                @block.scalar
                def _(act):
                    act.wait_ge(xT_d, 2)
                    act.activation(xT[:, :, bass.ds(ch * CH, CH)], xTc[:], ACT.Copy)
                    act.wait_ge(e_in, 1)
                    act.activation(sc[:, :, 0:E_ALL], sc[:, :, 0:E_ALL], ACT.Exp).then_inc(ac, 1)
                    act.wait_ge(e_in, 2)
                    act.activation(fm[:], fm[:], ACT.Exp).then_inc(ac, 1)

                @block.tensor
                def _(pe):
                    pe.wait_ge(xn_d, 1)
                    for k in range(2):
                        for i in range(CT):
                            ins = pe.transpose(bank(k)[:, i * P:(i + 1) * P], xn[:, i, k * P:(k + 1) * P], g["idf"][:])
                        ins.then_inc(pe_s, 1)
                    pe.wait_ge(xT_d, 2)
                    for i in range(CT):
                        for k in range(2):
                            ins = pe.matmul(bank(2)[:, i * E_ALL:(i + 1) * E_ALL], xTc[:, k, i * P:(i + 1) * P], gw[:, k, :],
                                            start=(k == 0), stop=(k == 1))
                    ins.then_inc(pe_s, 1)
                    pe.wait_ge(wd_d, 1)
                    for i in range(CT):
                        ins = pe.transpose(bank(3)[0:E_ALL + 2, i * P:(i + 1) * P], left[:, i, :], g["idf"][:])
                    ins.then_inc(pe_s, 1)
                    pe.wait_ge(wdT_d, 1)
                    for i in range(CT):
                        ins = pe.matmul(bank(4)[:, i * E_ALL:(i + 1) * E_ALL], wdT[:, i * P:(i + 1) * P], pick[:],
                                        start=True, stop=True)
                    ins.then_inc(pe_s, 1)
                    pe.wait_ge(pk_d, 1)
                    for i in range(CT):
                        ins = pe.transpose(bank(5)[0:E_ALL, i * P:(i + 1) * P], pk[:, i, :], g["idf"][:])
                    ins.then_inc(pe_s, 1)

                @block.sync
                def _(sp):
                    sp.wait_ge(wT_d, 1)
                    sp.dma_start(g["w_dram"][0:E_ALL, bass.ds(ch * CH, CH)], wTs[:]).then_inc(out_d, 16)
                    sp.wait_ge(wT_d, 2)
                    for e in range(EXPERTS):
                        sp.dma_start(g["wp_dram"][e, :, :, bass.ds(ch * CH, CH)].rearrange("a k n -> k a n"),
                                     parts[e * SLOTS:(e + 1) * SLOTS, :, :]).then_inc(out_d, 16)
                    sp.wait_ge(out_d, 16 * (1 + EXPERTS))
            clear(nc, sems)


def split(dve, c, hi, lo, x):
    c.link(dve.tensor_copy(hi, x))
    c.link(dve.tensor_tensor(lo, x, hi.bitcast(F32), ALU.subtract))


def experts(nc, g):
    bank, x1, xT = g["bank"], g["x1"], g["xT"]
    with ExitStack() as ctx:
        def sb(n, s, d=F32):
            return ctx.enter_context(nc.sbuf_tensor(n, s, d))
        sems = []

        def sem(n):
            sems.append(g["sems"][n])
            return sems[-1]

        W1 = [sb(f"W1_{j}", [P, 2, W1C]) for j in range(2)]
        W1hi = [sb(f"W1hi_{j}", [P, 2, W1C], F32R) for j in range(2)]
        W1lo = [sb(f"W1lo_{j}", [P, 2, W1C], F32R) for j in range(2)]
        xThi, xTlo = sb("xThi", [P, 2, TOK], F32R), sb("xTlo", [P, 2, TOK], F32R)
        split_done = sem("split_done")
        MU = [sb(f"MU_{j}", [P, 2, P]) for j in range(2)]
        QB = [sb(f"QB_{j}", [P, 3 * P]) for j in range(2)]
        QS = [sb(f"QS_{j}", [P, 3 * P]) for j in range(2)]
        DW = [sb(f"DW_{j}", [P, 2, D]) for j in range(2)]
        DS = [sb(f"DS_{j}", [P, D]) for j in range(2)]
        DA = [sb(f"DA_{j}", [P, 2, P]) for j in range(2)]
        WB = [sb(f"WB_{j}", [P, TOK]) for j in range(2)]
        WT = [sb(f"WT_{j}", [P, TOK], BF16) for j in range(2)]
        WM = [sb(f"WM_{j}", [P, W1C], BF16) for j in range(2)]
        sumw = [sb(f"sumw_{j}", [P, NTOK]) for j in range(2)]
        mu_w = sb("mu_w", [P, W1C])
        part = sb("part", [P, W1C], BF16)
        terms = sb("terms", [P, 3])
        aw = sb("aw", [P, CH])
        sg = sb("sg", [P, 2, CH])
        hh = [sb(f"hh_{j}", [P, 2, CH]) for j in range(2)]
        SHW = sb("SHW", [P, 2, 2 * SHARED])
        SHD = sb("SHD", [P, 3, D])
        sh_sg = sb("sh_sg", [P, 2, CH])
        shh = [sb(f"shh_{j}", [P, 3, CH]) for j in range(2)]
        w_in = [sem("w_in_a"), sem("w_in_b")]
        sh_in, dvc = sem("sh_in"), sem("e_dvc")
        wm_full, wm_read, wm_done, q_done = sem("wm_full"), sem("wm_read"), sem("wm_done"), sem("qb_done")
        a_full, aw_done, g_full = sem("a_full"), sem("aw_done"), sem("g_full")
        sg_done, h_done = sem("sg_done"), sem("h_done")
        d_full, dw_done, y_full, y_done = sem("d_full"), sem("dw_done"), sem("y_full"), sem("y_done")

        def load(sp, f, j):
            one = bass.ds(f, 1)
            for dst, name in ((W1[j], "w1T"), (MU[j], "muP"), (DW[j], "downT"), (DA[j], "down_qaT")):
                sp.dma_start(dst[:], g[name][one].rearrange("o p k n -> p (o k) n")).then_inc(w_in[j], 16)
            sp.dma_start(QB[j][:], g["qbT"][one].rearrange("o p n -> p (o n)")).then_inc(w_in[j], 16)
            sp.dma_start(QS[j][:], g["up_gate_scale"][one].rearrange("o n -> (o n)").partition_broadcast(P)).then_inc(w_in[j], 16)
            sp.dma_start(DS[j][64:P, :], g["down_scale"][one].rearrange("o n -> (o n)").partition_broadcast(64)
                         ).then_inc(w_in[j], 16)
            for s in range(2):
                sp.dma_start(WB[j][s * E_ALL:(s + 1) * E_ALL, :],
                             spread(g["w_dram"][bass.ds(f * SLOTS, SLOTS), :], 1, RANK)).then_inc(w_in[j], 16)
            r = 0
            for n in (3, 2, 1):
                sp.dma_start(WT[j][r:r + n * SLOTS, :], g["wp_dram"][one, 0:n].rearrange("o a k n -> (o a k) n")
                             ).then_inc(w_in[j], 16)
                r += n * SLOTS
        LOADS = 16 * (4 + 3 + 2 + 3)

        with nc.Block() as block:
            @block.sync
            def _(sp):
                sp.dma_start(SHW[:], g["sh_up_gateT"]).then_inc(sh_in, 16)
                sp.dma_start(SHD[:], g["sh_downT"]).then_inc(sh_in, 16)
                sp.dma_start(terms[:], g["term_rows"]).then_inc(sh_in, 16)
                sp.wait_ge(q_done, 1)
                sp.dma_start(g["w_dram"][E_ALL:, :], WB[0][0:SLOTS, :]).then_inc(sh_in, 16)
                sp.dma_start(g["wp_dram"][EXPERTS].rearrange("a k n -> (a k) n"), WT[0][0:3 * SLOTS, :]).then_inc(sh_in, 16)
                sp.wait_ge(sh_in, 80)

            @block.gpsimd
            def _(pool):
                for t in (WT[0][:], WT[1][:], hh[0][:], hh[1][:], WB[0][0:SLOTS, :]):
                    ins = pool.memset(t, 0.0)
                ins.then_inc(q_done, 1)

            @block.tensor
            def _(pe):
                pe.wait_ge(sh_in, 80)

                def gate_up(ch):
                    cols = slice(ch * CH, (ch + 1) * CH)
                    for i, (m, w) in enumerate(SH_T):
                        n = 3 * ch + i
                        if ch:
                            pe.wait_ge(h_done, n - 2)
                        for j in range(2):
                            for k in range(2):
                                ins = pe.matmul(bank(2 * i + j)[0:w, :], SHW[:, k, j * SHARED + m:j * SHARED + m + w],
                                                xT[:, k, cols], start=(k == 0), stop=(k == 1))
                        ins.then_inc(g_full, 1)
                gate_up(0)
                for ch in range(NCH):
                    if ch + 1 < NCH:
                        gate_up(ch + 1)
                    pe.wait_ge(h_done, 3 * ch + 3)
                    if ch:
                        pe.wait_ge(y_done, ch)
                    for i in range(CT):
                        for j, (m, w) in enumerate(SH_T):
                            ins = pe.matmul(bank(6 + i // 2)[:, (i % 2) * D:(i % 2 + 1) * D],
                                            shh[ch % 2][0:w, j, i * P:(i + 1) * P],
                                            SHD[0:w, j, :], start=(j == 0), stop=(j == 2))
                    ins.then_inc(y_full, 1)

            @block.scalar
            def _(act):
                for n in range(3 * NCH):
                    w = SH_T[n % 3][1]
                    act.wait_ge(g_full, n + 1)
                    if n >= 2:
                        act.wait_ge(h_done, n - 1)
                    act.activation(sh_sg[0:w, n % 2, :], bank(2 * (n % 3))[0:w, :], ACT.Silu).then_inc(sg_done, 1)

            @block.vector
            def _(dve):
                def hidden(ch):
                    for i, (m, w) in enumerate(SH_T):
                        n = 3 * ch + i
                        dve.wait_ge(sg_done, n + 1)
                        dve.tensor_tensor(shh[ch % 2][0:w, i, :], bank(2 * i + 1)[0:w, :], sh_sg[0:w, n % 2, :], ALU.mult
                                          ).then_inc(h_done, 1)
                c = Chain(dve, dvc)
                hidden(0)
                for ch in range(NCH):
                    cols = slice(ch * CH, (ch + 1) * CH)
                    split(dve, c, xThi[:, :, cols], xTlo[:, :, cols], xT[:, :, cols])
                    if ch + 1 < NCH:
                        hidden(ch + 1)
                    dve.wait_ge(y_full, ch + 1)
                    xs = x1[:, ch * CT:(ch + 1) * CT, :].rearrange("p t d -> p (t d)")
                    dve.tensor_tensor(xs, xs, g["pair"](3), ALU.add).then_inc(y_done, 1)
        clear(nc, sems)
        with nc.Block() as block:
            @block.sync
            def _(sp):
                load(sp, 0, 0)
                sp.wait_ge(w_in[0], LOADS)
        clear(nc, sems)

        UNITS = 2 * NCH
        G, U, BOTH, A, Y = 0, 1, 2, 6, 7

        def out_bank(n, i):
            return bank(3 * (n % 2) + i)

        with nc.Fori(0, EXPERTS // 2) as pair:
            with nc.Block() as block:
                @block.sync
                def _(sp):
                    load(sp, pair * 2 + 1, 1)
                    sp.wait_ge(y_full, 2 * NCH)
                    sp.wait_ge(q_done, 2)
                    load(sp, pair * 2 + 2, 0)
                    sp.wait_ge(w_in[1], LOADS)
                    sp.wait_ge(w_in[0], LOADS)

                @block.gpsimd
                def _(pool):
                    for j in range(2):
                        if j:
                            pool.wait_ge(w_in[1], LOADS)
                            pool.wait_ge(q_done, 2)
                        pool.tensor_tensor(QB[j][:], QB[j][:], QS[j][:], ALU.mult).then_inc(q_done, 1)
                        pool.wait_ge(q_done, 2 * j + 1)
                        pool.tensor_tensor(DW[j][64:P, 1, :], DW[j][64:P, 1, :], DS[j][64:P, :], ALU.mult).then_inc(q_done, 1)

                @block.tensor
                def _(pe):
                    def fold(j):
                        for k in range(2):
                            ins = pe.matmul(bank(A), MU[j][:, k, :], W1[j][:, k, :], start=(k == 0), stop=(k == 1))
                        ins.then_inc(wm_full, 1)

                    def low_in(n):
                        j, cols = n // NCH, slice(n % NCH * CH, (n % NCH + 1) * CH)
                        for t, (w, x) in enumerate(((W1hi[j], xThi), (W1hi[j], xTlo), (W1lo[j], xThi))):
                            for k in range(2):
                                pe.matmul(bank(A), w[:, k, 3 * P:4 * P], x[:, k, cols], start=(t + k == 0), stop=False)
                        pe.matmul(bank(A), WM[j][:, 3 * P:4 * P], WT[j][:, cols], start=False, stop=True).then_inc(a_full, 1)

                    def base(n):
                        j, cols = n // NCH, slice(n % NCH * CH, (n % NCH + 1) * CH)
                        for i in range(3):
                            for t, (w, x) in enumerate(((W1hi[j], xThi), (W1hi[j], xTlo), (W1lo[j], xThi))):
                                for k in range(2):
                                    pe.matmul(out_bank(n, i), w[:, k, i * P:(i + 1) * P], x[:, k, cols],
                                              start=(t + k == 0), stop=False)

                    def base_masks(n):
                        j, cols = n // NCH, slice(n % NCH * CH, (n % NCH + 1) * CH)
                        for i in range(3):
                            pe.matmul(out_bank(n, i), WM[j][:, i * P:(i + 1) * P], WT[j][:, cols], start=False, stop=False)

                    def mix(n):
                        pe.wait_ge(aw_done, n + 1)
                        for i in range(3):
                            ins = pe.matmul(out_bank(n, i), QB[n // NCH][:, i * P:(i + 1) * P], aw[:], start=False, stop=True)
                        ins.then_inc(g_full, 1)

                    def low_down(n):
                        pe.wait_ge(h_done, 2 * n + 2)
                        for k in range(2):
                            ins = pe.matmul(bank(A), DA[n // NCH][:, k, :], hh[n % 2][:, k, :], start=(k == 0), stop=(k == 1))
                        ins.then_inc(d_full, 1)

                    def down(n, half):
                        if 2 * n + half:
                            pe.wait_ge(y_done, 2 * n + half)
                        for i in (2 * half, 2 * half + 1):
                            for k in range(2):
                                ins = pe.matmul(bank(Y)[:, (i % 2) * D:(i % 2 + 1) * D], hh[n % 2][:, k, i * P:(i + 1) * P],
                                                DW[n // NCH][:, k, :], start=(k == 0), stop=(k == 1))
                        ins.then_inc(y_full, 1)

                    fold(0)
                    pe.wait_ge(split_done, 1)
                    base(0)
                    pe.wait_ge(wm_done, 1)
                    low_in(0)
                    base_masks(0)
                    pe.wait_ge(q_done, 1)
                    base(1)
                    base_masks(1)
                    mix(0)
                    low_in(1)
                    for n in range(UNITS):
                        if n + 1 < UNITS:
                            if n + 1 == NCH:
                                pe.wait_ge(q_done, 4)
                            mix(n + 1)
                        low_down(n)
                        if n + 2 == NCH:
                            pe.wait_ge(split_done, 2)
                        if n + 2 < UNITS:
                            base(n + 2)
                            if n + 2 == NCH:
                                pe.wait_ge(wm_done, 2)
                            base_masks(n + 2)
                        pe.wait_ge(dw_done, n + 1)
                        if n == 0:
                            pe.wait_ge(w_in[1], LOADS)
                            pe.wait_ge(q_done, 2)
                            fold(1)
                        down(n, 0)
                        if n == 0:
                            pe.wait_ge(wm_read, 2)
                        if n + 2 < UNITS:
                            low_in(n + 2)
                        down(n, 1)

                @block.scalar
                def _(act):
                    for n in range(UNITS):
                        act.wait_ge(g_full, n + 1)
                        if n:
                            act.wait_ge(h_done, 2 * n)
                        act.activation(sg[:, 0, :], out_bank(n, G), ACT.Silu).then_inc(sg_done, 1)
                        act.activation(sg[64:64 + I2, 1, :], out_bank(n, BOTH)[0:I2, :], ACT.Silu).then_inc(sg_done, 1)

                @block.vector
                def _(dve):
                    c = Chain(dve, dvc)

                    def split_w1(j):
                        c.link(dve.tensor_copy(W1hi[j][:], W1[j][:]))
                        dve.tensor_tensor(W1lo[j][:], W1[j][:], W1hi[j][:].bitcast(F32), ALU.subtract
                                          ).then_inc(split_done, 1)

                    def read_fold(j):
                        dve.wait_ge(wm_full, j + 1)
                        dve.tensor_copy(mu_w[:], bank(A)).then_inc(wm_read, 1)

                    def split_fold(j):
                        dve.wait_ge(wm_read, j + 1)
                        c.link(dve.tensor_copy(part[:], mu_w[:]))
                        c.did(dve.tensor_scalar(WM[j][:], part[:], terms[:, 0:1], None, ALU.mult))
                        c.link(dve.tensor_tensor(mu_w[:], mu_w[:], part[:], ALU.subtract))
                        c.link(dve.tensor_copy(part[:], mu_w[:]))
                        c.link(dve.tensor_tensor(mu_w[:], mu_w[:], part[:], ALU.subtract))
                        c.link(dve.scalar_tensor_tensor(WM[j][:], part[:], terms[:, 1:2], WM[j][:], ALU.mult, ALU.add))
                        dve.scalar_tensor_tensor(WM[j][:], mu_w[:], terms[:, 2:3], WM[j][:], ALU.mult, ALU.add
                                                 ).then_inc(wm_done, 1)

                    def weigh_low(n):
                        dve.wait_ge(a_full, n + 1)
                        dve.tensor_tensor(aw[:], bank(A), WB[n // NCH][:, n % NCH * CH:(n % NCH + 1) * CH], ALU.mult
                                          ).then_inc(aw_done, 1)

                    def hidden(n):
                        dve.wait_ge(sg_done, 2 * n + 1)
                        dve.tensor_tensor(hh[n % 2][:, 0, :], out_bank(n, U), sg[:, 0, :], ALU.mult).then_inc(h_done, 1)
                        dve.wait_ge(sg_done, 2 * n + 2)
                        dve.tensor_tensor(hh[n % 2][0:I2, 1, :], out_bank(n, BOTH)[64:64 + I2, :], sg[64:64 + I2, 1, :],
                                          ALU.mult).then_inc(h_done, 1)

                    def weigh_down(n):
                        dve.wait_ge(d_full, n + 1)
                        dve.tensor_tensor(hh[n % 2][64:P, 1, :], bank(A)[64:P, :],
                                          WB[n // NCH][64:P, n % NCH * CH:(n % NCH + 1) * CH], ALU.mult).then_inc(dw_done, 1)

                    def add(n, half):
                        dve.wait_ge(y_full, 2 * n + half + 1)
                        if n >= NCH:
                            dve.wait_ge(y_done, 2 * (n - NCH) + half + 1)
                        for i in (2 * half, 2 * half + 1):
                            t = n % NCH * CT + i
                            ins = dve.scalar_tensor_tensor(x1[:, t, :], bank(Y)[:, (i % 2) * D:(i % 2 + 1) * D],
                                                           sumw[n // NCH][:, t:t + 1], x1[:, t, :], ALU.mult, ALU.add)
                        ins.then_inc(y_done, 1)

                    for j in range(2):
                        c.did(dve.tensor_copy(sumw[j][:], g["sums"][:, :, bass.ds(pair * 2 + j, 1)]
                                              .rearrange("p t o -> p (t o)")))
                    split_w1(0)
                    read_fold(0)
                    split_fold(0)
                    weigh_low(0)
                    dve.wait_ge(g_full, 1)
                    weigh_low(1)
                    hidden(0)
                    for n in range(UNITS):
                        if n + 1 < UNITS:
                            hidden(n + 1)
                        weigh_down(n)
                        if n == 0:
                            read_fold(1)
                        add(n, 0)
                        if n + 2 < UNITS:
                            weigh_low(n + 2)
                        add(n, 1)
                        if n == 0:
                            split_w1(1)
                            split_fold(1)
            clear(nc, sems)


def build(nc, a, out):
    g = dict(a)
    with ExitStack() as ctx:
        def sb(n, s, d=F32):
            return ctx.enter_context(nc.sbuf_tensor(n, s, d))
        psum = ctx.enter_context(nc.psum_tensor("psum", [P, 8, 512], F32))
        g["bank"] = lambda n: psum[:, n, :]
        g["pair"] = lambda n: psum[:, 2 * n:2 * n + 2, :].rearrange("p a n -> p (a n)")
        g["w_dram"] = nc.dram_tensor("w_dram", (E_ALL + SLOTS, TOK), F32).ap()
        g["wp_dram"] = nc.dram_tensor("wp_dram", (EXPERTS + 1, 3, SLOTS, TOK), BF16).ap()
        g["sems"] = {n: ctx.enter_context(nc.semaphore(n)) for n in SEMAPHORES}
        g["x1"] = sb("x1", [P, NTOK, D])
        idf, idb, row = sb("idf", [P, P]), sb("idb", [P, P], BF16), sb("row", [P, 1])
        g.update(idf=idf, idb=idb, row=row)
        loaded, cast, stored, x_in = [ctx.enter_context(nc.semaphore(n)) for n in ("c_loaded", "c_cast", "stored", "x_in")]
        with ExitStack() as actx:
            ab = lambda n, s, d=F32: actx.enter_context(nc.sbuf_tensor(n, s, d))
            wq, wkv, wo = ab("wq", [P, 2, D]), ab("wkv", [P, 2, 2, 2 * D]), ab("wo", [P, 2, D])
            bq, gq, bo = ab("bq", [P, D]), ab("gq", [P, D]), ab("bo", [P, D])
            bkv, gk = ab("bkv", [P, 3, 2 * D]), ab("gk", [P, 3, D])
            vmask, is_img, is_txt = ab("vmask", [P, S_ALL]), ab("is_img", [P, NT_ALL]), ab("is_txt", [P, NT_ALL])
            ln, isfew = ab("ln", [P, 1], I32), ab("isfew", [P, 1], I32)
            lf, lg = ab("lf", [P, 1]), ab("lg", [P, 1])
            pairs = [(idf[:], a["ident"]), (row[:], a["row_no"]), (wq[:], a["wqT"]), (wkv[:], a["wkvT"]), (wo[:], a["woT"]),
                     (bq[:], a["bq"].partition_broadcast(P)), (gq[:], a["gq"].partition_broadcast(P)),
                     (bo[:], a["bo"].partition_broadcast(P)), (vmask[:], a["vmask"]), (is_img[:], a["is_img"]),
                     (is_txt[:], a["is_txt"]), (ln[:], a["lens"].partition_broadcast(P))]
            for k, (lo, hi, which) in enumerate(((0, P, 0), (0, P, 1), (0, P, 1))):
                pairs.append((bkv[:, k, :], a["bkv"][which].partition_broadcast(P)))
                pairs.append((gk[:, k, :], a["gk"][which].partition_broadcast(P)))
            x_norm = ab("x_norm", [P, NTOK, 2])
            bn, vr, tx = ab("bn", [P, NTOK, 6]), ab("vr", [P, NTOK]), ab("tx", [P, NTOK])
            rx = ab("rx", [P, NTOK])
            with nc.Block() as block:
                @block.sync
                def _(sp):
                    sp.dma_start(g["x1"][:], a["x"].rearrange("b (t p) d -> p (b t) d", p=P)).then_inc(x_in, 16)
                    for dst, src in pairs:
                        sp.dma_start(dst, src).then_inc(loaded, 16)
                    sp.wait_ge(loaded, 16 * len(pairs))
                    sp.dma_start(bkv[0:1, 1, :], a["bkv"][0:1]).then_inc(stored, 16)
                    sp.dma_start(gk[0:1, 1, :], a["gk"][0:1]).then_inc(stored, 16)
                    sp.wait_ge(stored, 32)

                @block.vector
                def _(dve):
                    c = Chain(dve, cast)
                    dve.wait_ge(x_in, 16)
                    for t in range(NTOK):
                        c.did(dve.bn_stats(bn[:, t, :], g["x1"][:, t, :]))
                    c.need(c.n)
                    for t in range(NTOK):
                        c.did(dve.bn_aggr(x_norm[:, t, :], bn[:, t, :]))
                    c.need(c.n)
                    c.link(dve.tensor_scalar(vr[:], x_norm[:, :, 1], EPS_LN, None, ALU.add))
                    rsqrt(dve, c, rx[:], vr[:], tx[:])
                    c.did(dve.tensor_copy(x_norm[:, :, 1], rx[:]))
                    dve.wait_ge(loaded, 16 * len(pairs))
                    c.did(dve.tensor_copy(idb[:], idf[:]))
                    c.link(dve.tensor_copy(lf[:], ln[:]))
                    c.link(dve.tensor_scalar(lg[:], lf[:], 1.0, None, ALU.is_ge))
                    c.link(dve.tensor_scalar(lf[:], lf[:], float(SHORT_LEN), None, ALU.is_le))
                    c.link(dve.tensor_tensor(isfew[:], lf[:], lg[:], ALU.mult))
            clear(nc, [loaded, cast, stored, x_in])
            g.update(x_norm=x_norm, wq=wq, wkv=wkv, wo=wo, bq=bq, gq=gq, bo=bo, bkv=bkv, gk=gk, vmask=vmask, is_img=is_img,
                     is_txt=is_txt, len=ln)
            few = nc.values_load(isfew[0:1, 0:1], min_val=0, max_val=1)
            with nc.If(few > 0):
                attention(nc, g, NT_SHORT, "few")
            with nc.Else():
                attention(nc, g, NT_ALL, "all")
        with ExitStack() as ectx:
            g["xT"] = ectx.enter_context(nc.sbuf_tensor("xT", [P, 2, TOK], F32))
            g["sums"] = ectx.enter_context(nc.sbuf_tensor("sums", [P, NTOK, EXPERTS], F32))
            routing(nc, g, ctx)
            experts(nc, g)
        with nc.Block() as block:
            @block.sync
            def _(sp):
                sp.dma_start(out.rearrange("b (t p) d -> p (b t) d", p=P), g["x1"][:]).then_inc(stored, 16)
                sp.wait_ge(stored, 16)


def lay_out(i):
    f = lambda n: np.ascontiguousarray(i[n])
    z = lambda *s: np.zeros(s, np.float32)
    halves = lambda w: np.ascontiguousarray(w.reshape(w.shape[:-2] + (w.shape[-2] // P, P, w.shape[-1])).swapaxes(-3, -2))
    o = {"x": f("x")}
    c = f("ctx_2048").transpose(0, 2, 1)
    slots = z(B, D, S_ALL, P)
    for k in range(NT_ALL):
        part = c[:, :, k * P:(k + 1) * P]
        if k == MIXED:
            slots[:, :, k, 0:1] = part[:, :, 0:1]
            slots[:, :, k + 1, 1:] = part[:, :, 1:]
        else:
            slots[:, :, k + (k > MIXED), 0:part.shape[2]] = part
    o["ctxT"] = np.ascontiguousarray(slots.reshape(B, 2, P, S_ALL, P).transpose(0, 2, 3, 1, 4)).reshape(B, P, -1)
    L = "L0_xattn_"
    o["wqT"], o["woT"] = halves(f(L + "Wq")), halves(f(L + "Wo"))
    wkv = np.stack([np.concatenate([f(L + "Wk_img"), f(L + "Wv_img")], 1), np.concatenate([f(L + "Wk"), f(L + "Wv")], 1)])
    o["wkvT"] = np.ascontiguousarray(halves(wkv).transpose(1, 0, 2, 3))
    o["bq"], o["gq"], o["bo"], o["lens"] = f(L + "bq"), f(L + "gq"), f(L + "bo"), f(L + "context_lens")
    o["bkv"] = np.stack([np.concatenate([f(L + "bk_img"), f(L + "bv_img")]), np.concatenate([f(L + "bk"), f(L + "bv")])])
    o["gk"] = np.stack([f(L + "gk_img"), f(L + "gk")])
    tok = np.arange(NT_ALL * P)
    o["ident"] = np.eye(P, dtype=np.float32)
    o["row_no"] = np.arange(P, dtype=np.float32)[:, None]
    rows = z(EXTRA, NT_ALL * P)
    rows[0] = np.where(tok < IMG, -FAR, np.where(tok < CTX, tok - IMG, FAR))
    rows[1:4] = tok < IMG
    rows[4:7] = tok >= IMG
    o["key_rows"] = rows
    o["is_img"] = np.ascontiguousarray((tok < IMG).astype(np.float32).reshape(NT_ALL, P).T)
    o["is_txt"] = np.ascontiguousarray((tok >= IMG).astype(np.float32).reshape(NT_ALL, P).T)
    real = (tok < CTX).astype(np.float32).reshape(NT_ALL, P).T
    vm = np.concatenate([real[:, :MIXED + 1], real[:, MIXED:]], 1)
    vm[:, MIXED], vm[:, MIXED + 1] = o["is_img"][:, MIXED], o["is_txt"][:, MIXED]
    o["vmask"] = np.ascontiguousarray(vm)
    E = "L0_ffn_"
    o["gate_wT"] = halves(f(E + "gate_weight").T)
    o["inv"] = f(E + "inv_mapping").reshape(-1)
    gT, uT = f(E + "gate_W").transpose(0, 2, 1), f(E + "up_W").transpose(0, 2, 1)
    qa = lambda n: f(E + n).reshape(EXPERTS, E_ALL, -1).transpose(0, 2, 1)
    w1 = z(EXPERTS, D, W1C)
    w1[:, :, 0:P], w1[:, :, P:2 * P] = gT[:, :, 0:P], uT[:, :, 0:P]
    w1[:, :, 2 * P:2 * P + I2], w1[:, :, 2 * P + 64:2 * P + 64 + I2] = gT[:, :, P:], uT[:, :, P:]
    w1[:, :, 3 * P:3 * P + 64], w1[:, :, 3 * P + 64:] = qa("gate_qa"), qa("up_qa")
    o["w1T"] = halves(w1)
    mu, rows = z(EXPERTS, D, P), z(P, 3)
    for t, (a, _) in enumerate(TERMS):
        mu[:, :, t * SLOTS:(t + 1) * SLOTS] = f(E + "mask_up_W")
        rows[t * SLOTS:(t + 1) * SLOTS, a] = 1
    o["muP"], o["term_rows"] = halves(mu), rows
    qb = lambda n: f(E + n).transpose(0, 1, 3, 2).reshape(EXPERTS, E_ALL, -1)
    q = z(EXPERTS, P, 3 * P)
    q[:, 0:64, 0:P], q[:, 64:, P:2 * P] = qb("gate_qb")[:, :, 0:P], qb("up_qb")[:, :, 0:P]
    q[:, 0:64, 2 * P:2 * P + I2], q[:, 64:, 2 * P + 64:2 * P + 64 + I2] = qb("gate_qb")[:, :, P:], qb("up_qb")[:, :, P:]
    o["qbT"] = q
    s = z(EXPERTS, 3 * P)
    gs, us = f(E + "gate_scale"), f(E + "up_scale")
    s[:, 0:P], s[:, P:2 * P], s[:, 2 * P:2 * P + I2], s[:, 2 * P + 64:2 * P + 64 + I2] = gs[:, 0:P], us[:, 0:P], gs[:, P:], us[:, P:]
    o["up_gate_scale"] = s

    def pad(w, rows):
        p = z(w.shape[0], rows, w.shape[2])
        p[:, 0:w.shape[1]] = w
        return halves(p)
    d = z(EXPERTS, 2 * P, D)
    d[:, 0:INTER], d[:, 2 * P - E_ALL:] = f(E + "down_W").transpose(0, 2, 1), qb("down_qb")
    o["downT"] = halves(d)
    d = z(EXPERTS, INTER, P)
    d[:, :, P - E_ALL:] = qa("down_qa")
    o["down_qaT"] = pad(d, 2 * P)
    o["down_scale"] = f(E + "down_scale")
    o["sh_up_gateT"] = halves(np.concatenate([f(E + "sh_gate_W").T, f(E + "sh_up_W").T], 1))
    o["sh_downT"] = pad(f(E + "sh_down_W").T[None], 3 * P)[0]
    for n in ("w1T", "muP", "qbT", "up_gate_scale", "downT", "down_qaT", "down_scale"):
        o[n] = np.concatenate([o[n], np.zeros_like(o[n][:1])])
    return {k: np.ascontiguousarray(v) for k, v in o.items()}


def kernel(**inputs):
    import concourse.bacc as bacc
    from concourse.bass_utils import run_bass_kernel_spmd

    nc = bacc.Bacc("TRN2", target_bir_lowering=False, num_devices=1)
    arrays = {f"in_{k}": v for k, v in lay_out(inputs).items()}
    a = {k[3:]: nc.dram_tensor(k, v.shape, mybir.dt.from_np(v.dtype), kind="ExternalInput").ap() for k, v in arrays.items()}
    out = nc.dram_tensor("out", (B, SQ, D), F32, kind="ExternalOutput").ap()
    build(nc, a, out)
    return run_bass_kernel_spmd(nc, [arrays], core_ids=[0]).results[0]["out"]
```
